# Optimizing a Trainium2 kernel written in Bass

```python
import numpy as np
import jax
import jax.numpy as jnp

def _softmax(x, axis=-1):
    return jax.nn.softmax(x, axis=axis)
def _gelu(x):
    return jax.nn.gelu(x, approximate=True)
def _silu(x):
    return jax.nn.silu(x)
def _sigmoid(x):
    return jax.nn.sigmoid(x)
def _layernorm(x, axis=-1, eps=1e-5):
    m = jnp.mean(x, axis=axis, keepdims=True)
    v = jnp.var(x, axis=axis, keepdims=True)
    return (x - m) / jnp.sqrt(v + eps)
def _scatter_add(tgt, idx, src, axis=0):
    return tgt.at[idx].add(src)
def _segment_sum(src, seg, n):
    return jax.ops.segment_sum(src, seg, n)

kernel_name = 'mk_conv_preact_d2_conv_nchw256_8f5d54'

def setup_inputs(seed: int = 0):
    np.random.seed(seed)
    _w = jnp.asarray
    def _rec_inputs():
        import jax
        import jax.numpy as jnp
        _gk = jax.random.key(seed)
        x = -0.0002023 + 1 * jax.random.normal(jax.random.fold_in(_gk, 1), (8, 256, 56, 56), jnp.float32)
        return x
    x = _rec_inputs()
    def _L0_conv_setup():
        import jax, jax.numpy as jnp
        import numpy as np
        C = 256
        K = 7
        GS = 4
        G = C // GS
        RC = C // 2
        OC = K * K * G
        B, H, W = (8, 56, 56)
        key = jax.random.key(seed)
        k0, k1, k2, k3, k4 = jax.random.split(key, 5)
        x = jax.random.normal(k0, (B, C, H, W), jnp.float32)
        w1 = jax.random.normal(k1, (RC, C), jnp.float32) / np.sqrt(C).astype(np.float32)
        b1 = jax.random.normal(k2, (RC,), jnp.float32) * 0.01
        w2 = jax.random.normal(k3, (OC, RC), jnp.float32) / np.sqrt(RC).astype(np.float32)
        b2 = jax.random.normal(k4, (OC,), jnp.float32) * 0.01
        return {'x': x, 'w1': w1, 'b1': b1, 'w2': w2, 'b2': b2}
    _L0_conv_all = _L0_conv_setup()
    _L0_conv_in = {k: v for k, v in _L0_conv_all.items() if k in ('w1', 'b1', 'w2', 'b2', )}
    del _L0_conv_all

    def _L1_conv_setup():
        import jax, jax.numpy as jnp
        import numpy as np
        ACT_BITS = 8
        Q_B = 2 ** (ACT_BITS - 1)
        EPS = 1e-06
        GN_EPS = 1e-05
        SCALE = 0.01
        STRIDE = 1
        PADDING = 1

        def _group_norm_1group(x, gamma, beta):
            mean = jnp.mean(x, axis=(1, 2, 3), keepdims=True)
            var = jnp.var(x, axis=(1, 2, 3), keepdims=True)
            xn = (x - mean) * jax.lax.rsqrt(var + GN_EPS)
            return xn * gamma[None, :, None, None] + beta[None, :, None, None]
        key = jax.random.key(seed)
        k1, k2 = jax.random.split(key)
        x = jax.random.normal(k1, (16, 256, 64, 64), dtype=jnp.float32)
        weight = jax.random.normal(k2, (256, 256, 3, 3), dtype=jnp.float32)
        bias = jnp.zeros((256,), dtype=jnp.float32)
        ln_weight = jnp.ones((256,), dtype=jnp.float32)
        ln_bias = jnp.zeros((256,), dtype=jnp.float32)
        return {'x': x, 'weight': weight, 'bias': bias, 'ln_weight': ln_weight, 'ln_bias': ln_bias}
    _L1_conv_all = _L1_conv_setup()
    _L1_conv_in = {k: v for k, v in _L1_conv_all.items() if k in ('weight', 'bias', 'ln_weight', 'ln_bias', )}
    del _L1_conv_all

    return {
        "x": x,
        "L0_conv_w1": _L0_conv_in["w1"],
        "L0_conv_b1": _L0_conv_in["b1"],
        "L0_conv_w2": _L0_conv_in["w2"],
        "L0_conv_b2": _L0_conv_in["b2"],
        "L1_conv_weight": _L1_conv_in["weight"],
        "L1_conv_bias": _L1_conv_in["bias"],
        "L1_conv_ln_weight": _L1_conv_in["ln_weight"],
        "L1_conv_ln_bias": _L1_conv_in["ln_bias"],
    }

def reference(x, L0_conv_w1, L0_conv_b1, L0_conv_w2, L0_conv_b2, L1_conv_weight, L1_conv_bias, L1_conv_ln_weight, L1_conv_ln_bias):
    import jax
    import jax.numpy as jnp
    def _L0_conv_ref(x, w1, b1, w2, b2):
        import jax, jax.numpy as jnp
        import numpy as np
        C = 256
        K = 7
        GS = 4
        G = C // GS
        RC = C // 2
        OC = K * K * G
        B, H, W = (8, 56, 56)
        b, _, h, w = x.shape
        wt_in = jax.lax.stop_gradient(x)
        wt = jnp.einsum('oc,bchw->bohw', w1, wt_in) + b1[None, :, None, None]
        wt = jnp.einsum('oc,bchw->bohw', w2, wt) + b2[None, :, None, None]
        wt = wt.reshape(b, G, K * K, h, w)
        pad = (K - 1) // 2
        xp = jnp.pad(x, ((0, 0), (0, 0), (pad, pad), (pad, pad)))
        xg = xp.reshape(b, G, GS, h + 2 * pad, w + 2 * pad)
        out = jnp.zeros((b, G, GS, h, w), x.dtype)
        for p in range(K * K):
            ki, kj = divmod(p, K)
            out = out + wt[:, :, p][:, :, None] * xg[:, :, :, ki:ki + h, kj:kj + w]
        return out.reshape(b, C, h, w)

    def _L1_conv_ref(x, weight, bias, ln_weight, ln_bias):
        import jax, jax.numpy as jnp
        import numpy as np
        ACT_BITS = 8
        Q_B = 2 ** (ACT_BITS - 1)
        EPS = 1e-06
        GN_EPS = 1e-05
        SCALE = 0.01
        STRIDE = 1
        PADDING = 1

        def _group_norm_1group(x, gamma, beta):
            mean = jnp.mean(x, axis=(1, 2, 3), keepdims=True)
            var = jnp.var(x, axis=(1, 2, 3), keepdims=True)
            xn = (x - mean) * jax.lax.rsqrt(var + GN_EPS)
            return xn * gamma[None, :, None, None] + beta[None, :, None, None]
        x_ln = _group_norm_1group(x, ln_weight, ln_bias)
        gamma = jnp.maximum(jnp.max(jnp.abs(x_ln)), EPS)
        x_scaled = x_ln * (Q_B / gamma)
        x_clipped = jnp.clip(x_scaled, -Q_B + EPS, Q_B - EPS)
        x_quant = jnp.round(x_clipped)
        delta = 0.7 * jnp.mean(jnp.abs(weight))
        w_q = jnp.where(weight > delta, SCALE, jnp.where(weight < -delta, -SCALE, 0.0)).astype(weight.dtype)
        y = jax.lax.conv_general_dilated(x_quant, w_q, window_strides=(STRIDE, STRIDE), padding=[(PADDING, PADDING), (PADDING, PADDING)], dimension_numbers=('NCHW', 'OIHW', 'NCHW'), feature_group_count=1)
        y = y * (gamma / Q_B) + bias[None, :, None, None]
        return y

    def _gn(v, G=32, eps=1e-5):
        B_, C_, H_, W_ = v.shape
        g = v.reshape(B_, G, C_ // G, H_, W_)
        m = jnp.mean(g, axis=(2, 3, 4), keepdims=True)
        s = jnp.var(g, axis=(2, 3, 4), keepdims=True)
        return ((g - m) / jnp.sqrt(s + eps)).reshape(v.shape)

    def _ln_c(v, eps=1e-6):
        m = jnp.mean(v, axis=1, keepdims=True)
        s = jnp.var(v, axis=1, keepdims=True)
        return (v - m) / jnp.sqrt(s + eps)

    def _ln_t(v, eps=1e-5):
        m = jnp.mean(v, axis=-1, keepdims=True)
        s = jnp.var(v, axis=-1, keepdims=True)
        return (v - m) / jnp.sqrt(s + eps)

    def _to_tokens(v):
        B_, C_, H_, W_ = v.shape
        return v.reshape(B_, C_, H_ * W_).transpose(0, 2, 1)
    def _from_tokens(t, like):
        B_, C_, H_, W_ = like.shape
        return t.transpose(0, 2, 1).reshape(B_, C_, H_, W_)

    x = x + _L0_conv_ref(_gn(x), L0_conv_w1, L0_conv_b1, L0_conv_w2, L0_conv_b2)
    x = x + _L1_conv_ref(_gn(x), L1_conv_weight, L1_conv_bias, L1_conv_ln_weight, L1_conv_ln_bias)
    return x


_drawn_inputs = setup_inputs


def setup_inputs(seed=0):
    import zlib

    import numpy as np

    out = dict(_drawn_inputs(seed))
    spreads = {'L1_conv_bias': (0.0, 0.54),
     'L1_conv_ln_weight': (1.0, 0.6),
     'L1_conv_ln_bias': (0.0, 0.8)}
    factors = {'L0_conv_b1': 5.81, 'L0_conv_b2': 5.704}
    for name, (base, spread) in spreads.items():
        noise = np.random.default_rng([zlib.crc32(name.encode()), seed]).standard_normal(out[name].shape)
        drawn = base * np.exp(spread * noise) if base else spread * noise
        out[name] = jnp.asarray(drawn.astype(out[name].dtype))
    for name, factor in factors.items():
        out[name] = (out[name] * factor).astype(out[name].dtype)
    return out
```

```python
from contextlib import ExitStack

import numpy as np

import concourse.bass as bass
from concourse import mybir

B, C, HW = 8, 256, 56
PIX = HW * HW
RC = 128
K, PAD = 7, 3
TAPS = K * K
PW = HW + 2 * PAD
PN = PW * PW
ROWS = 8
NK = HW // ROWS
PX = ROWS * HW
PCH = ROWS * PW
STEPS = 2 * NK
VROWS = PW - 3
HLEN = PN - 3
G = C // 4
GN_EPS = 1e-5
Q_B = 128.0
MAGIC = 1.5 * 2.0 ** 23
CW = HW + 2
CN = CW * CW
KK = 9
TILES = 2 * NK

QUADS = ([("H", r, 0) for r in (0, 1, 2)] + [("V", 0, c) for c in (4, 5, 6)]
         + [("H", r, 3) for r in (4, 5, 6)] + [("V", 3, c) for c in (0, 1, 2)])
CENTRE = 12
DQ = [0, 1, 3, 4, 6, 7, 9, 10]
PQ = [2, 5, 8, 11]
ND, NP = len(DQ), len(PQ)
NS = NP + 1
DRING, PRING = 4, 2


def quad_taps(q):
    if q == CENTRE:
        return [PAD * K + PAD] * 4
    kind, r, c = QUADS[q]
    return [(r * K + c + s) if kind == "H" else ((r + s) * K + c) for s in range(4)]


def build(nc, x, w1, b1, w2, b2, cw, cbias, lnw, lnb, ident_d, sel_d, mask_d, out):
    f32 = mybir.dt.float32
    bf16 = mybir.dt.bfloat16
    ALU = mybir.AluOpType
    ACT = mybir.ActivationFunctionType
    AX = mybir.AxisListType.X

    xs = x.rearrange("b (h g s) r w -> b h s g (r w)", h=2, s=4)
    outs = out.rearrange("b (h g s) r w -> b h s g (r w)", h=2, s=4)
    xn_d = nc.dram_tensor("xn_padded", (B, C, PN), f32).ap()
    xns = xn_d.rearrange("b (h g s) n -> b h s g n", h=2, s=4)
    t_d = nc.dram_tensor("t_all", (B, RC, PIX), f32).ap()
    x1_d = nc.dram_tensor("x1_all", (B, 2, 128, PIX), f32).ap()
    wq_d = nc.dram_tensor("wq_all", (128, 4 * KK * 128), bf16).ap()

    nc.disable_value_cache = True
    ctx = ExitStack()
    with ctx:
        def sb(name, shape, dt=f32):
            return ctx.enter_context(nc.sbuf_tensor(name, shape, dt))

        def ps(name, shape):
            return ctx.enter_context(nc.psum_tensor(name, shape, f32))

        def sem(name):
            return ctx.enter_context(nc.semaphore(name))

        def counts(value):
            return not isinstance(value, int) or value > 0

        def view(ap, dims):
            return bass.AP(ap.tensor, ap.offset, [list(ap.ap[0])] + dims)

        shift_rows = sb("shift_rows", [128, 4, VROWS * PW])
        shift_cols = sb("shift_cols", [128, 4, HLEN])
        prod = sb("prod", [128, DRING + PRING, 4 * PX])
        w2T = sb("w2T", [128, 2, 13, 128])
        w1T = sb("w1T", [128, 2, 128])
        wt_sb = sb("wt_sb", [128, 2, PX])
        t_in = sb("t_in", [128, 2, PX])
        xres = sb("xres", [128, 2, PX])
        xc = sb("xc", [128, 2, PCH])
        raw = sb("raw", [128, 2, 2, PX])
        xn = sb("xn", [128, 2, PCH])
        t_out = sb("t_out", [128, PX])
        mask = sb("mask", [128, 128])
        ones = sb("ones", [128, 128])
        sel = sb("sel", [128, 32])
        b2c = sb("b2c", [128, 26])
        cols = sb("cols", [128, 8])
        b1c, lnw_c, lnb_c, bias_c = cols[:, 0:1], cols[:, 1:3], cols[:, 3:5], cols[:, 5:7]
        st0 = sb("st0", [128, 2, NK, 6])
        cf = sb("cf", [128, 32])
        st1 = sb("st1", [128, B * STEPS, 6])
        mx1 = sb("mx1", [128, B * STEPS])
        mn1 = sb("mn1", [128, B * STEPS])

        H = shift_cols[:, :, :].rearrange("p a b -> p (a b)")
        V = shift_rows[:, :, :].rearrange("p a b -> p (a b)")
        P = prod[:, :, :].rearrange("p a b -> p (a b)")
        w2_raw = H[0:G, 0:TAPS * 128]
        b2_row = H[0:1, 6272:6272 + TAPS * G]
        w1_raw = H[:, 9408:9408 + C]
        w1_ordered = H[:, 9664:9664 + C]
        ident = P[:, 9216:9344]
        ident_b = P[:, 9344:9408].bitcast(bf16)
        zeros = V[:, 0:16 * PAD * PW]
        cw_raw = P[:, 0:2 * C * KK]
        wq = P[:, 4608:6912].bitcast(bf16)
        wneg = P[:, 6912:9216].bitcast(bf16)
        wq_ordered = P[:, 0:2304].bitcast(bf16)
        wqT_stage = wneg

        wt_ps = ps("wt_ps", [128, DRING, 512])
        sb_ps = ps("sb_ps", [128, 512])
        acc_ps = ps("acc_ps", [128, 2, 512])
        misc_ps = ps("misc_ps", [128, 512])

        const_in = sem("const_in")
        w2_in = sem("w2_in")
        cw_in = sem("cw_in")
        zero_set = sem("zero_set")
        zero_stored = sem("zero_stored")
        ones_set = sem("ones_set")
        setup_ps = sem("setup_ps")
        setup_sb = sem("setup_sb")
        abs_sum = sem("abs_sum")
        abs_ps = sem("abs_ps")
        wq_ready = sem("wq_ready")
        wq_ps = sem("wq_ps")
        wq_sb = sem("wq_sb")
        wq_stored = sem("wq_stored")
        chain0 = sem("chain0")
        chain1 = sem("chain1")
        raw_in = [sem(f"raw_in{p}") for p in range(2)]
        stat_done = sem("stat_done")
        coef_in = sem("coef_in")
        coef_ps = sem("coef_ps")
        var_ready = sem("var_ready")
        std_ready = sem("std_ready")
        coef_done = sem("coef_done")
        norm_done = sem("norm_done")
        t_ps = sem("t_ps")
        t_ready = sem("t_ready")
        xn_stored = sem("xn_stored")
        t_stored = sem("t_stored")
        tin_in = [sem(f"tin_in{p}") for p in range(2)]
        xc_in = [sem(f"xc_in{p}") for p in range(2)]
        xres_in = [sem(f"xres_in{p}") for p in range(2)]
        shift_in = [sem(f"shift_in{k}") for k in range(NK)]
        d_made = sem("d_made")
        s_made = sem("s_made")
        d_biased = sem("d_biased")
        s_biased = sem("s_biased")
        d_mult = sem("d_mult")
        centre_mult = sem("centre_mult")
        s_used = sem("s_used")
        d_added = sem("d_added")
        p_added = sem("p_added")
        x1_ready = sem("x1_ready")
        x1_stats = sem("x1_stats")
        x1_stored = sem("x1_stored")
        gsum_in = sem("gsum_in")
        gsum_ps = sem("gsum_ps")
        gstd = sem("gstd")
        affine_ready = sem("affine_ready")
        border_set = sem("border_set")
        wq_in = sem("wq_in")
        x1_in = [sem(f"x1_in{p}") for p in range(2)]
        ident_in = sem("ident_in")
        shown_ready = sem("shown_ready")
        act_q = sem("act_q")
        q_ready = sem("q_ready")
        conv_done = sem("conv_done")
        y_scaled = sem("y_scaled")
        y_ready = sem("y_ready")
        y_stored = [sem(f"y_stored{p}") for p in range(4)]

        def linker(eng, s, base):
            n = [0]

            def link(ins):
                n[0] += 1
                ins.then_inc(s, 1)
                eng.wait_ge(s, base + n[0])
            return link

        def shifted(q, k):
            kind, r, c = QUADS[q]
            buf, pitch = (shift_cols, HLEN) if kind == "H" else (shift_rows, VROWS * PW)
            a = buf[:, 0, (ROWS * k + r) * PW + c:(ROWS * k + r) * PW + c + 1]
            return view(a, [[pitch, 4], [PW, ROWS], [1, HW]])

        def broadcast(wt):
            return view(wt, [[0, 4], [HW, ROWS], [1, HW]])

        def product(n):
            return view(prod[:, n % DRING, 0:1], [[PX, 4], [HW, ROWS], [1, HW]])

        def pool_product(n):
            return view(prod[:, DRING + n % PRING, 0:1], [[PX, 4], [HW, ROWS], [1, HW]])

        ORDER = [("D", 0), ("D", 1), ("S", 0), ("D", 2), ("S", 1), ("D", 3), ("S", 2), ("D", 4), ("D", 5), ("S", 3),
                 ("D", 6), ("D", 7), ("S", 4)]

        def quad_of(kind, n):
            return DQ[n] if kind == "D" else (PQ[n - 1] if n else CENTRE)

        def x1b(par):
            return V[:, par * 2 * PIX:(par + 1) * 2 * PIX].rearrange("p (h n) -> p h n", h=2)

        XQ = CN
        def xq(par):
            return H[:, par * XQ:(par + 1) * XQ].bitcast(bf16).rearrange("p (h n) -> p h n", h=2)

        HALF = PIX // 2
        def qtmp(q):
            return H[:, 2 * XQ + (q % 2) * HALF:2 * XQ + (q % 2 + 1) * HALF]

        wqT = H[:, 2 * XQ + 2 * HALF:2 * XQ + 2 * HALF + 2 * KK * 128].bitcast(bf16)

        ident2 = xc[:, 0, 0:128]

        def ybuf(slot):
            return prod[:, slot, 0:PX]

        def conv_bank(t):
            return wt_ps[:, t, 0:PX]

        block = ctx.enter_context(nc.Block())

        @block.sync
        def _(sp):
            def load_raw(b, j):
                if j >= 2 and j - 2 < NK:
                    if counts(b * NK + (j - 2) + 1):
                        sp.wait_ge(stat_done, b * NK + (j - 2) + 1)
                elif j >= 2:
                    if counts(b * NK + (j - 2 - NK) + 1):
                        sp.wait_ge(norm_done, b * NK + (j - 2 - NK) + 1)
                else:
                    if counts(b * NK - 1 + j):
                        sp.wait_ge(norm_done, b * NK - 1 + j)
                k = j % NK
                for h in range(2):
                    sp.dma_start(raw[:, j % 2, h, :], xs[b, h, :, :, k * PX:(k + 1) * PX]).then_inc(raw_in[j % 2], 16)

            def store_norm(b, k):
                sp.wait_ge(norm_done, b * NK + k + 1)
                o = (ROWS * k + PAD) * PW
                for h in range(2):
                    sp.dma_start(xns[b, h, :, :, o:o + PCH], xn[:, h, :]).then_inc(xn_stored, 16)
                sp.wait_ge(t_ready, b * NK + k + 1)
                sp.dma_start(t_d[b, :, k * PX:(k + 1) * PX], t_out[:, :]).then_inc(t_stored, 16)

            def load_shifted(b, h, k, first=False):
                sp.wait_ge(xn_stored, (b * NK + k + 1) * 32)
                o = k * PCH
                nv = PCH if k < NK - 1 else VROWS * PW - o
                nh = PCH if k < NK - 1 else HLEN - o
                src = xn_d[b, h * 128:(h + 1) * 128, :]
                for s in range(4):
                    p = slice(32 * s, 32 * s + 32)
                    for dst, n, d in ((shift_rows, nv, s * PW), (shift_cols, nh, s)):
                        sp.dma_start(dst[p, :, o:o + n], src[:, o + d:o + d + n].rearrange("(g q) n -> g q n", q=4)
                                     ).then_inc(shift_in[k], 16)

            def load_step(b, i):
                h, k = divmod(i, NK)
                sp.wait_ge(t_stored, (b * NK + k + 1) * 16)
                sp.dma_start(t_in[:, i % 2, :], t_d[b, :, k * PX:(k + 1) * PX]).then_inc(tin_in[i % 2], 16)
                sp.wait_ge(xn_stored, (b * NK + k + 1) * 32)
                o = (ROWS * k + PAD) * PW
                sp.dma_start(xc[:, i % 2, :], xns[b, h, :, :, o:o + PCH]).then_inc(xc_in[i % 2], 16)

            def load_xres(b, i):
                h, k = divmod(i, NK)
                sp.dma_start(xres[:, i % 2, :], xs[b, h, :, :, k * PX:(k + 1) * PX]).then_inc(xres_in[i % 2], 16)

            def store_x1(b, i):
                h, k = divmod(i, NK)
                s = b * STEPS + i
                sp.wait_ge(x1_ready, s + 1)
                sp.dma_start(x1_d[b, h, :, k * PX:(k + 1) * PX], xres[:, i % 2, :]).then_inc(x1_stored, 16)

            def image(b, first, last):
                for i in range(STEPS):
                    s = b * STEPS + i
                    if not last:
                        load_raw(b + 1, i)
                    if counts(s * ND):
                        sp.wait_ge(d_mult, s * ND)
                    if counts(s * NS):
                        sp.wait_ge(s_used, s * NS)
                    if not (last and i == STEPS - 1):
                        load_step(*((b, i + 1) if i + 1 < STEPS else (b + 1, 0)))
                    if i == 0 and not first:
                        load_shifted(b, 0, NK - 1)
                    elif 1 <= i <= NK:
                        load_shifted(b, 1, i - 1)
                    elif i > NK and not last:
                        load_shifted(b + 1, 0, i - NK - 1)
                    if not (first and i == 0):
                        store_x1(*((b, i - 1) if i else (b - 1, STEPS - 1)))
                    if not (last and i == STEPS - 1):
                        if counts(s):
                            sp.wait_ge(x1_stats, s)
                        if counts(s * 16):
                            sp.wait_ge(x1_stored, s * 16)
                        load_xres(*((b, i + 1) if i + 1 < STEPS else (b + 1, 0)))
                    if i >= NK and not last:
                        store_norm(b + 1, i - NK)

            for dst, src in ((sel[:, :], sel_d), (mask[:, :], mask_d), (ident, ident_d), (w1_raw, w1),
                             (b1c, b1.rearrange("(p o) -> p o", o=1))):
                sp.dma_start(dst, src).then_inc(const_in, 16)
            for dst, src in ((lnw_c, lnw), (lnb_c, lnb), (bias_c, cbias)):
                v = src.rearrange("(h g s o) -> h s g o", h=2, s=4, o=1)
                for h in range(2):
                    sp.dma_start(dst[:, h:h + 1], v[h], allow_slow_non_contiguous=True).then_inc(const_in, 16)
            sp.dma_start(w2_raw.rearrange("g (p r) -> g p r", r=128), w2.rearrange("(g p) r -> g p r", p=TAPS)).then_inc(w2_in, 16)
            sp.dma_start(b2_row, b2.rearrange("(a n) -> a n", a=1)).then_inc(w2_in, 16)
            sp.wait_ge(zero_set, 1)
            allrows = xn_d.rearrange("b c n -> (b c) n").rearrange("(p q) n -> p q n", q=16)
            for o in (0, PN - PAD * PW):
                sp.dma_start(allrows[:, :, o:o + PAD * PW], zeros.rearrange("p (q n) -> p q n", q=16)).then_inc(zero_stored, 16)
            for j in range(STEPS):
                load_raw(0, j)
                if j > NK:
                    store_norm(0, j - NK - 1)
            store_norm(0, NK - 1)
            sp.wait_ge(zero_stored, 32)
            sp.wait_ge(setup_sb, 9)
            for k in range(NK):
                load_shifted(0, 0, k)
            load_step(0, 0)
            load_xres(0, 0)
            image(0, True, False)
            with sp.Fori(1, B - 1) as b:
                image(b, False, False)
            image(B - 1, False, True)
            store_x1(B - 1, STEPS - 1)

            def load_x1(b, par):
                for h in range(2):
                    sp.dma_start(x1b(par)[:, h, :], x1_d[b, h, :, :]).then_inc(x1_in[par], 16)

            sp.wait_ge(d_mult, B * STEPS * ND)
            sp.wait_ge(s_used, B * STEPS * NS)
            sp.wait_ge(x1_stored, B * STEPS * 16)
            sp.wait_ge(wq_stored, 16)
            sp.dma_start(ident2, ident_d).then_inc(ident_in, 16)
            load_x1(0, 0)
            sp.dma_start(wqT, wq_d).then_inc(wq_in, 16)
            load_x1(1, 1)

            def stores(b, par, more):
                for n in range(TILES):
                    k, m = divmod(n, 2)
                    slot = (TILES * par + n) % 4
                    sp.wait_ge(y_ready, b * TILES + n + 1)
                    sp.dma_start(outs[b, m, :, :, k * PX:(k + 1) * PX], ybuf(slot)).then_inc(y_stored[slot], 16)
                if more:
                    load_x1(b + 2, par)

            for par in range(2):
                stores(par, par, True)
            with sp.Fori(1, B // 2 - 1) as j:
                for par in range(2):
                    stores(j * 2 + par, par, True)
            for par in range(2):
                stores(B - 2 + par, par, False)
            for slot in range(4):
                sp.wait_ge(y_stored[slot], B * TILES // 4 * 16)

        @block.vector
        def _(dve):
            v = nc.vector
            NL0 = 13

            def stats(b, k):
                dve.wait_ge(raw_in[k % 2], (b * NK + k // 2 + 1) * 32)
                v.bn_stats(st0[:, 0, k, :], raw[:, k % 2, 0, :])
                v.bn_stats(st0[:, 1, k, :], raw[:, k % 2, 1, :]).then_inc(stat_done, 1)

            def coef_a(b):
                link = linker(dve, chain0, b * NL0)
                dve.wait_ge(stat_done, (b + 1) * NK)
                v.memset(cf[:, 31:32], 0.0)
                v.bn_aggr(cf[:, 20:22], st0[:, 0, :, :])
                link(v.bn_aggr(cf[:, 22:24], st0[:, 1, :, :]))
                link(v.tensor_copy(cf[:, 0:2], cf[:, 20:24:2]))
                link(v.tensor_tensor(cf[:, 16:18], cf[:, 0:2], cf[:, 0:2], ALU.mult))
                v.tensor_tensor(cf[:, 2:4], cf[:, 16:18], cf[:, 21:24:2], ALU.add).then_inc(coef_in, 1)

            def coef_b(b):
                link = linker(dve, chain0, b * NL0 + 3)
                dve.wait_ge(coef_ps, b + 1)
                link(v.tensor_copy(cf[:, 4:8], misc_ps[:, 0:4]))
                link(v.tensor_tensor(cf[:, 16:18], cf[:, 4:6], cf[:, 4:6], ALU.mult))
                link(v.tensor_tensor(cf[:, 18:20], cf[:, 6:8], cf[:, 16:18], ALU.subtract))
                v.tensor_scalar_add(cf[:, 8:10], cf[:, 18:20], GN_EPS).then_inc(var_ready, 1)

            def newton(link, var, root, inv, tmp, last):
                link(v.reciprocal(inv, root))
                link(v.tensor_tensor(tmp, inv, inv, ALU.mult))
                link(v.tensor_tensor(tmp, tmp, var, ALU.mult))
                link(v.tensor_scalar(tmp, tmp, -0.5, 1.5, ALU.mult, ALU.add))
                last(v.tensor_tensor(inv, inv, tmp, ALU.mult))

            def coef_c(b):
                link = linker(dve, chain0, b * NL0 + 6)
                dve.wait_ge(std_ready, b + 1)
                if counts(b * NK):
                    dve.wait_ge(norm_done, b * NK)
                newton(link, cf[:, 8:10], cf[:, 10:12], cf[:, 12:14], cf[:, 16:18], link)
                link(v.tensor_tensor(cf[:, 18:20], cf[:, 4:6], cf[:, 12:14], ALU.mult))
                link(v.tensor_scalar_mul(cf[:, 14:16], cf[:, 18:20], -1.0))
                v.nop().then_inc(coef_done, 1)

            def finish(b, i):
                s = b * STEPS + i
                dve.wait_ge(d_added, (s + 1) * ND)
                dve.wait_ge(p_added, (s + 1) * NP)
                dve.wait_ge(s_used, s * NS + 1)
                v.tensor_tensor(xres[:, i % 2, :], acc_ps[:, i % 2, 0:PX], xres[:, i % 2, :], ALU.add).then_inc(x1_ready, 1)
                dve.wait_ge(x1_ready, s + 1)
                at = s if isinstance(s, int) else None
                one = slice(at, at + 1) if at is not None else bass.ds(s, 1)
                v.tensor_reduce(mx1[:, one], xres[:, i % 2, :], AX, ALU.max)
                v.tensor_reduce(mn1[:, one], xres[:, i % 2, :], AX, ALU.min)
                v.bn_stats(st1[:, one, :].rearrange("p a b -> p (a b)"), xres[:, i % 2, :]).then_inc(x1_stats, 1)

            def image(b, first, last):
                for i in range(STEPS):
                    k = i % NK
                    s = b * STEPS + i
                    phase = b * 2 + i // NK
                    for n in range(ND):
                        if n == 0:
                            for kk in (k, k + 1)[:2 if k + 1 < NK else 1]:
                                dve.wait_ge(shift_in[kk], (phase + 1) * 128)
                        dve.wait_ge(d_biased, s * ND + n + 1)
                        if counts(s * ND + n + 1 - DRING):
                            dve.wait_ge(d_added, s * ND + n + 1 - DRING)
                        v.tensor_tensor(product(n), broadcast(wt_ps[:, n % DRING, 0:PX]), shifted(DQ[n], k), ALU.mult
                                        ).then_inc(d_mult, 1)
                        if n == 1 and not (first and i == 0):
                            finish(*((b, i - 1) if i else (b - 1, STEPS - 1)))
                        if last:
                            continue
                        if n == 0 and i == NK:
                            coef_b(b + 1)
                        if n == 3 and i == NK:
                            coef_c(b + 1)
                        if n == 5 and i < NK:
                            stats(b + 1, i)
                        if n == 5 and i == NK - 1:
                            coef_a(b + 1)

            v.memset(zeros, 0.0).then_inc(zero_set, 1)
            v.memset(ones[:, :], 1.0)
            v.memset(xn[:, :, :], 0.0).then_inc(ones_set, 1)
            if counts(11 * 16):
                dve.wait_ge(const_in, 11 * 16)
            v.tensor_copy(ident_b, ident).then_inc(ones_set, 1)
            for h in range(2):
                last_copy = v.tensor_copy(view(w1_ordered[:, h * 128:h * 128 + 1], [[32, 4], [1, 32]]),
                                          view(w1_raw[:, h * 128:h * 128 + 1], [[1, 4], [4, 32]]))
            last_copy.then_inc(ones_set, 1)
            where = {t: [(q, s) for q in range(13) for s, u in enumerate(quad_taps(q)) if u == t] for t in range(TAPS)}
            for r in range(K):
                dve.wait_ge(setup_ps, r + 1)
                for c in range(K):
                    src = wt_ps[:, r % 4, c * G:(c + 1) * G].rearrange("p (h g) -> p h g", h=2)
                    for q, s in where[r * K + c]:
                        last_copy = v.tensor_copy(w2T[:, :, q, 32 * s:32 * s + 32], src)
                last_copy.then_inc(setup_sb, 1)
            dve.wait_ge(setup_ps, 8)
            v.tensor_copy(b2c[:, :], sb_ps[:, 0:26]).then_inc(setup_sb, 1)
            dve.wait_ge(setup_ps, 9)
            v.tensor_copy(w1T[:, :, :].rearrange("p a b -> p (a b)"), acc_ps[:, 0, 0:256]).then_inc(setup_sb, 1)
            for k in range(NK):
                stats(0, k)
            coef_a(0)
            coef_b(0)
            coef_c(0)
            dve.wait_ge(cw_in, 32)
            v.tensor_reduce(cf[:, 24:25], cw_raw, AX, ALU.add, apply_absolute_value=True).then_inc(abs_sum, 1)
            dve.wait_ge(abs_ps, 1)
            wl = linker(dve, chain1, 0)
            wl(v.tensor_scalar(cf[:, 25:26], sb_ps[:, 64:65], 1.0 / (C * C * KK), 0.7, ALU.mult, ALU.mult))
            wl(v.tensor_scalar_mul(cf[:, 26:27], cf[:, 25:26], -1.0))
            wl(v.tensor_scalar(wq, cw_raw, cf[:, 25:26], None, ALU.is_gt))
            wl(v.tensor_scalar(wneg, cw_raw, cf[:, 26:27], None, ALU.is_lt))
            for mk in range(4):
                o = mk * KK * 128
                src = [view(a[:, o:o + 1], [[KK, 4], [4 * KK, 32], [1, KK]]) for a in (wq, wneg)]
                ins = v.tensor_tensor(view(wq_ordered[:, o:o + 1], [[32, 4], [1, 32], [128, KK]]), src[0], src[1], ALU.subtract)
            ins.then_inc(wq_ready, 1)
            dve.wait_ge(wq_stored, 16)

            image(0, True, False)
            with dve.Fori(1, B - 1) as b:
                image(b, False, False)
            image(B - 1, False, True)
            finish(B - 1, STEPS - 1)

            link = linker(dve, chain1, 4)
            NI = 2 * B
            ag = raw[:, 0, 0, 0:2 * NI].rearrange("p (n t) -> p n t", t=2)
            g2 = raw[:, 0, 0, 64:64 + 2 * NI]
            w = [raw[:, 0, 1, NI * n:NI * (n + 1)] for n in range(24)]
            gm, gv, root, rg, tmp, dd, e1, e2, aa, bb, mxr, mnr = w[:12]
            us, uu = w[12], w[13]
            cand = raw[:, 1, 0, 0:2 * NI]
            small = raw[:, 1, 1, :]
            dve.wait_ge(x1_stats, B * STEPS)
            dve.wait_ge(norm_done, B * NK)
            for n in range(NI):
                link(v.bn_aggr(ag[:, n, :], st1[:, n * NK:(n + 1) * NK, :]))
            link(v.tensor_reduce(mxr, mx1[:, :].rearrange("p (n k) -> p n k", k=NK), AX, ALU.max))
            link(v.tensor_reduce(mnr, mn1[:, :].rearrange("p (n k) -> p n k", k=NK), AX, ALU.min))
            link(v.tensor_copy(g2[:, 0:NI], ag[:, :, 0]))
            link(v.tensor_tensor(tmp, g2[:, 0:NI], g2[:, 0:NI], ALU.mult))
            link(v.tensor_tensor(g2[:, NI:2 * NI], tmp, ag[:, :, 1], ALU.add))
            v.nop().then_inc(gsum_in, 1)
            dve.wait_ge(gsum_ps, 1)
            link(v.tensor_copy(gm, misc_ps[:, 0:NI]))
            link(v.tensor_tensor(tmp, gm, gm, ALU.mult))
            link(v.tensor_tensor(gv, misc_ps[:, NI:2 * NI], tmp, ALU.subtract))
            link(v.tensor_scalar_add(gv, gv, GN_EPS))
            v.nop().then_inc(gsum_in, 1)
            dve.wait_ge(gstd, 1)
            newton(link, gv, root, rg, tmp, link)
            link(v.tensor_tensor(dd, g2[:, 0:NI], gm, ALU.subtract))
            link(v.tensor_tensor(e1, dd, rg, ALU.mult))
            link(v.tensor_tensor(e2, dd, dd, ALU.mult))
            link(v.tensor_tensor(e2, e2, ag[:, :, 1], ALU.add))
            link(v.tensor_tensor(e2, e2, rg, ALU.mult))
            link(v.tensor_tensor(e2, e2, rg, ALU.mult))
            link(v.tensor_tensor(us[:, 0:B], e1[:, 0:NI:2], e1[:, 1:NI:2], ALU.add))
            link(v.tensor_tensor(us[:, B:2 * B], e2[:, 0:NI:2], e2[:, 1:NI:2], ALU.add))
            v.nop().then_inc(gsum_in, 1)
            dve.wait_ge(gsum_ps, 2)
            link(v.tensor_scalar_mul(uu, misc_ps[:, 64:64 + 2 * B], 1.0 / C))
            mu, v2 = uu[:, 0:B], uu[:, B:2 * B]
            link(v.tensor_tensor(tmp[:, 0:B], mu, mu, ALU.mult))
            link(v.tensor_tensor(v2, v2, tmp[:, 0:B], ALU.subtract))
            link(v.tensor_scalar_add(v2, v2, GN_EPS))
            v.nop().then_inc(gsum_in, 1)
            dve.wait_ge(gstd, 2)
            r2 = w[14][:, 0:B]
            newton(link, v2, small[:, 0:B], r2, tmp[:, 0:B], link)

            def per_image(a):
                return view(a, [[1, B], [0, 2]])

            def per_half(a):
                return view(a, [[0, B], [1, 2]])

            def three(a):
                return view(a, [[2, B], [1, 2]])

            link(v.tensor_tensor(three(aa), three(rg), per_image(r2), ALU.mult))
            link(v.tensor_tensor(three(aa), three(aa), per_half(lnw_c), ALU.mult))
            link(v.tensor_tensor(tmp, gm, rg, ALU.mult))
            link(v.tensor_tensor(three(tmp), three(tmp), per_image(mu), ALU.add))
            link(v.tensor_tensor(three(tmp), three(tmp), per_image(r2), ALU.mult))
            link(v.tensor_tensor(three(tmp), three(tmp), per_half(lnw_c), ALU.mult))
            link(v.tensor_tensor(three(bb), per_half(lnb_c), three(tmp), ALU.subtract))
            for n, ext in enumerate((mxr, mnr)):
                c = cand[:, n * NI:(n + 1) * NI]
                link(v.tensor_tensor(c, aa, ext, ALU.mult))
                link(v.tensor_tensor(c, c, bb, ALU.add))
            link(v.tensor_reduce(small[:, 16:17], cand, AX, ALU.max, apply_absolute_value=True))
            v.nop().then_inc(gsum_in, 1)
            dve.wait_ge(gsum_ps, 3)
            link(v.tensor_reduce(small[0:1, 17:18], misc_ps[0:1, 128:256], AX, ALU.max))
            link(v.tensor_scalar_max(small[0:1, 18:19], small[0:1, 17:18], 1e-6))
            v.nop().then_inc(gsum_in, 1)
            dve.wait_ge(gsum_ps, 4)
            gam, rq, ys = small[:, 19:20], small[:, 20:21], small[:, 21:22]
            link(v.tensor_copy(gam, misc_ps[:, 256:257]))
            link(v.reciprocal(rq, gam))
            link(v.tensor_scalar_mul(rq, rq, Q_B))
            link(v.tensor_scalar(ys, gam, 1.0 / Q_B, 0.01, ALU.mult, ALU.mult))
            link(v.tensor_scalar(aa, aa, rq, None, ALU.mult))
            link(v.tensor_scalar(bb, bb, rq, None, ALU.mult))
            v.nop().then_inc(affine_ready, 1)
            for par in range(2):
                link(v.memset(H[:, par * XQ:(par + 1) * XQ], 0.0))

            NQ = 8
            def quantise(b, q, par):
                h, half = divmod(q, 2)
                lq = linker(dve, chain0, B * NL0 + b * NQ + 2 * q)
                dve.wait_ge(act_q, b * 4 + q + 1)
                if q == 0:
                    if counts((b - 1) * TILES):
                        dve.wait_ge(conv_done, (b - 1) * TILES)
                lq(v.tensor_scalar(qtmp(q), qtmp(q), MAGIC, MAGIC, ALU.add, ALU.subtract))
                inner = xq(par)[:, h, :].rearrange("p (r c) -> p r c", c=CW)[:, 1 + 28 * half:29 + 28 * half, 1:1 + HW]
                lq(v.tensor_scalar(inner, qtmp(q).rearrange("p (r c) -> p r c", c=HW), Q_B, -Q_B, ALU.min, ALU.max))
                v.nop().then_inc(q_ready, 1)

            def outputs(b, par, more):
                for n in range(TILES):
                    k, m = divmod(n, 2)
                    slot = (TILES * par + n) % 4
                    dve.wait_ge(y_scaled, b * TILES + n + 1)
                    v.tensor_tensor(ybuf(slot), ybuf(slot), x1b(par)[:, m, k * PX:(k + 1) * PX], ALU.add).then_inc(y_ready, 1)
                    if more and n in (1, 3, 5, 7):
                        quantise(b + 1, n // 2, 1 - par)

            for q in range(4):
                quantise(0, q, 0)
            for par in range(2):
                outputs(par, par, True)
            with dve.Fori(1, B // 2 - 1) as j:
                for par in range(2):
                    outputs(j * 2 + par, par, True)
            for par in range(2):
                outputs(B - 2 + par, par, par == 0)

        @block.gpsimd
        def _(pool):
            g = nc.gpsimd

            def image(b, first, last):
                for i in range(STEPS):
                    k = i % NK
                    s = b * STEPS + i
                    phase = b * 2 + i // NK
                    par = i % 2
                    wt = wt_sb[:, i % 2, :]
                    pool.wait_ge(s_biased, s * NS + 1)
                    pool.wait_ge(xc_in[par], (b * NK + i // 2 + 1) * 16)
                    rows = lambda a: a.rearrange("p (r c) -> p r c", c=HW)
                    centre = xc[:, par, :].rearrange("p (r c) -> p r c", c=PW)[:, :, PAD:PAD + HW]
                    g.tensor_tensor(rows(wt), rows(wt), centre, ALU.mult).then_inc(centre_mult, 1)
                    pool.wait_ge(centre_mult, s + 1)
                    pool.wait_ge(xres_in[par], (b * NK + i // 2 + 1) * 16)
                    g.tensor_tensor(xres[:, par, :], xres[:, par, :], wt, ALU.add).then_inc(s_used, 1)
                    for kk in (k, k + 1)[:2 if k + 1 < NK else 1]:
                        pool.wait_ge(shift_in[kk], (phase + 1) * 128)
                    for n in range(NP):
                        pool.wait_ge(s_biased, s * NS + n + 2)
                        if counts(s * NP + n + 1 - PRING):
                            pool.wait_ge(p_added, s * NP + n + 1 - PRING)
                        g.tensor_tensor(pool_product(n), broadcast(wt_sb[:, (i + n + 1) % 2, :]), shifted(PQ[n], k), ALU.mult
                                        ).then_inc(s_used, 1)

            pool.wait_ge(wq_stored, 16)
            image(0, True, False)
            with pool.Fori(1, B - 1) as b:
                image(b, False, False)
            image(B - 1, False, True)

        @block.scalar
        def _(act):
            a = nc.scalar

            def normalise(b, k):
                j = NK + k
                act.wait_ge(coef_done, b + 1)
                act.wait_ge(raw_in[j % 2], (b * NK + j // 2 + 1) * 32)
                if counts((b * NK + k) * 32):
                    act.wait_ge(xn_stored, (b * NK + k) * 32)
                if counts(b * NK + k):
                    act.wait_ge(t_ps, b * NK + k)
                for h in range(2):
                    inner = xn[:, h, :].rearrange("p (r c) -> p r c", c=PW)[:, :, PAD:PAD + HW]
                    ins = a.activation(inner, raw[:, j % 2, h, :].rearrange("p (r c) -> p r c", c=HW), ACT.Identity,
                                       bias=cf[:, 14 + h:15 + h], scale=cf[:, 12 + h:13 + h])
                ins.then_inc(norm_done, 1)

            def bias_t(b, k):
                act.wait_ge(t_ps, b * NK + k + 1)
                if counts((b * NK + k) * 16):
                    act.wait_ge(t_stored, (b * NK + k) * 16)
                a.activation(t_out[:, :], misc_ps[:, 0:PX], ACT.Identity, bias=b1c).then_inc(t_ready, 1)

            def root(b):
                act.wait_ge(var_ready, b + 1)
                a.activation(cf[:, 10:12], cf[:, 8:10], ACT.Sqrt).then_inc(std_ready, 1)

            def image(b, first, last):
                for i in range(STEPS):
                    h = i // NK
                    s = b * STEPS + i
                    for kind, n in ORDER:
                        q = quad_of(kind, n)
                        bias = b2c[:, h * 13 + q:h * 13 + q + 1]
                        if kind == "D":
                            act.wait_ge(d_made, s * ND + n + 1)
                            w = wt_ps[:, n % DRING, 0:PX]
                            a.activation(w, w, ACT.Identity, bias=bias).then_inc(d_biased, 1)
                        else:
                            act.wait_ge(s_made, s * NS + n + 1)
                            if counts(s * NS + n - 1):
                                act.wait_ge(s_used, s * NS + n - 1)
                            a.activation(wt_sb[:, (i + n) % 2, :], sb_ps[:, 0:PX], ACT.Identity, bias=bias).then_inc(s_biased, 1)
                        if last:
                            continue
                        if (kind, n) == ("D", 3) and i == NK:
                            root(b + 1)
                        if (kind, n) == ("D", 5) and i >= NK:
                            normalise(b + 1, i - NK)
                    if not last and i >= NK:
                        bias_t(b + 1, i - NK)

            cws = cw.rearrange("(m g s) i a b -> m s g (i a b)", m=2, s=4)
            for m in range(2):
                act.dma_start(cw_raw[:, m * C * KK:(m + 1) * C * KK], cws[m]).then_inc(cw_in, 16)
            root(0)
            act.wait_ge(ones_set, 1)
            act.wait_ge(setup_sb, 9)
            for k in range(NK):
                normalise(0, k)
                bias_t(0, k)
            for r in range(5):
                n = 1024 if r < 4 else 512
                act.wait_ge(wq_ps, r + 1)
                a.activation(wqT_stage[:, r * 1024:r * 1024 + n], wt_ps[:, r % 4, :].bitcast(bf16)[:, 0:n], ACT.Copy).then_inc(wq_sb, 1)
            act.wait_ge(wq_sb, 5)
            act.dma_start(wq_d, wqT_stage).then_inc(wq_stored, 16)
            image(0, True, False)
            with act.Fori(1, B - 1) as b:
                image(b, False, False)
            image(B - 1, False, True)

            NI = 2 * B
            w = [raw[:, 0, 1, NI * n:NI * (n + 1)] for n in range(24)]
            small = raw[:, 1, 1, :]
            act.wait_ge(gsum_in, 2)
            a.activation(w[2], w[1], ACT.Sqrt).then_inc(gstd, 1)
            act.wait_ge(gsum_in, 4)
            a.activation(small[:, 0:B], w[13][:, B:2 * B], ACT.Sqrt).then_inc(gstd, 1)
            aa, bb, ys = raw[:, 0, 1, 8 * NI:9 * NI], raw[:, 0, 1, 9 * NI:10 * NI], small[:, 21:22]

            def affine_of(b, pairs, q, par):
                h, half = divmod(q, 2)
                act.wait_ge(x1_in[par], (pairs + 1) * 32)
                if counts(b * 4 + q - 1):
                    act.wait_ge(q_ready, b * 4 + q - 1)
                c = b * 2 + h
                one = slice(c, c + 1) if isinstance(c, int) else bass.ds(c, 1)
                src = x1b(par)[:, h, half * HALF:(half + 1) * HALF]
                a.activation(qtmp(q), src, ACT.Identity, bias=shown[:, 1, h:h + 1], scale=shown[:, 0, h:h + 1]).then_inc(act_q, 1)

            shown = raw[:, 1, 0, 64:68].rearrange("p (t h) -> p t h", t=2)

            def show(b, pairs):
                c = b * 2
                two = slice(c, c + 2) if isinstance(c, int) else bass.ds(c, 2)
                if counts(b * 4):
                    act.wait_ge(act_q, b * 4)
                a.activation(shown[:, 0, :], aa[:, two], ACT.Copy)
                a.activation(shown[:, 1, :], bb[:, two], ACT.Copy).then_inc(shown_ready, 1)
                act.wait_ge(shown_ready, b + 1)

            def outputs(b, pairs, par, more):
                for n in range(TILES):
                    k, m = divmod(n, 2)
                    tile = TILES * par + n
                    slot = tile % 4
                    act.wait_ge(conv_done, b * TILES + n + 1)
                    if counts((pairs * (2 * TILES // 4) + tile // 4) * 16):
                        act.wait_ge(y_stored[slot], (pairs * (2 * TILES // 4) + tile // 4) * 16)
                    a.activation(ybuf(slot), conv_bank(slot), ACT.Identity, bias=bias_c[:, m:m + 1], scale=ys).then_inc(y_scaled, 1)
                    if more and n in (0, 2, 4, 6):
                        if n == 0:
                            show(b + 1, pairs + par)
                        affine_of(b + 1, pairs + par, n // 2, 1 - par)

            act.wait_ge(affine_ready, 1)
            show(0, 0)
            for q in range(4):
                affine_of(0, 0, q, 0)
            for par in range(2):
                outputs(par, 0, par, True)
            with act.Fori(1, B // 2 - 1) as j:
                for par in range(2):
                    outputs(j * 2 + par, j, par, True)
            for par in range(2):
                outputs(B - 2 + par, B // 2 - 1, par, par == 0)

        @block.tensor
        def _(pe):
            mm = nc.tensor.matmul

            def group_mean(b):
                pe.wait_ge(coef_in, b + 1)
                if counts(b * NK):
                    pe.wait_ge(t_ready, b * NK)
                mm(misc_ps[:, 0:4], mask[:, :], cf[:, 0:4], start=True, stop=True).then_inc(coef_ps, 1)

            def make_t(b, k):
                pe.wait_ge(norm_done, b * NK + k + 1)
                if counts(b * NK + k):
                    pe.wait_ge(t_ready, b * NK + k)
                for h in range(2):
                    inner = xn[:, h, :].rearrange("p (r c) -> p r c", c=PW)[:, :, PAD:PAD + HW]
                    ins = mm(misc_ps[:, 0:PX], w1T[:, h, :], inner, start=h == 0, stop=h == 1)
                ins.then_inc(t_ps, 1)

            def make(b, i, kind, n):
                s = b * STEPS + i
                if (kind, n) == ("D", 0):
                    pe.wait_ge(tin_in[i % 2], (b * NK + i // 2 + 1) * 16)
                lhsT = w2T[:, i // NK, quad_of(kind, n), :]
                if kind == "D":
                    if counts(s * ND + n + 1 - DRING):
                        pe.wait_ge(d_mult, s * ND + n + 1 - DRING)
                    mm(wt_ps[:, n % DRING, 0:PX], lhsT, t_in[:, i % 2, :], start=True, stop=True).then_inc(d_made, 1)
                else:
                    if counts(s * NS + n):
                        pe.wait_ge(s_biased, s * NS + n)
                    mm(sb_ps[:, 0:PX], lhsT, t_in[:, i % 2, :], start=True, stop=True).then_inc(s_made, 1)

            def add(b, i, kind, n, start, stop):
                s = b * STEPS + i
                if kind == "D":
                    pe.wait_ge(d_mult, s * ND + n + 1)
                    buf, done = n % DRING, d_added
                else:
                    pe.wait_ge(s_used, s * NS + n + 2)
                    buf, done = DRING + n % PRING, p_added
                if start:
                    if counts(s - 1):
                        pe.wait_ge(x1_ready, s - 1)
                for j in range(4):
                    ins = mm(acc_ps[32 * j:32 * j + 32, i % 2, 0:PX], sel[:, :], prod[:, buf, j * PX:(j + 1) * PX],
                             start=start, stop=stop)
                ins.then_inc(done, 1)

            SEQ = [("w", 0, "D", 3), ("a", "D", 0), ("w", 0, "S", 2), ("w", 0, "D", 4), ("a", "D", 1), ("w", 0, "D", 5),
                   ("a", "D", 2), ("a", "P", 0), ("w", 0, "S", 3), ("w", 0, "D", 6), ("a", "D", 3), ("w", 0, "D", 7),
                   ("a", "D", 4), ("a", "P", 1), ("w", 0, "S", 4), ("w", 1, "D", 0), ("a", "D", 5), ("t",),
                   ("w", 1, "D", 1), ("a", "D", 6), ("a", "P", 2), ("w", 1, "S", 0), ("w", 1, "D", 2),
                   ("a", "D", 7), ("a", "P", 3), ("w", 1, "S", 1)]

            def image(b, first, last):
                for i in range(STEPS):
                    if i == NK and not last:
                        group_mean(b + 1)
                    for e in SEQ:
                        if e[0] == "t":
                            if i >= NK and not last:
                                make_t(b + 1, i - NK)
                        elif e[0] == "a":
                            add(b, i, e[1], e[2], e[1:] == ("D", 0), e[1:] == ("P", 3))
                        elif e[1] == 0:
                            make(b, i, e[2], e[3])
                        elif i + 1 < STEPS:
                            make(b, i + 1, e[2], e[3])
                        elif not last:
                            make(b + 1, 0, e[2], e[3])

            if counts(11 * 16):
                pe.wait_ge(const_in, 11 * 16)
            pe.wait_ge(w2_in, 32)
            for r in range(K):
                if counts(r - 3):
                    pe.wait_ge(setup_sb, r - 3)
                for c in range(K):
                    t = r * K + c
                    ins = nc.tensor.transpose(wt_ps[:, r % 4, c * G:(c + 1) * G], w2_raw[:, t * 128:(t + 1) * 128], ident[0:G, 0:G])
                ins.then_inc(setup_ps, 1)
            pe.wait_ge(ones_set, 1)
            for h in range(2):
                for q in range(13):
                    taps = quad_taps(q)
                    for j in range(4):
                        o = h * 32 * TAPS + taps[j]
                        ins = mm(sb_ps[32 * j:32 * j + 32, h * 13 + q:h * 13 + q + 1], view(b2_row[:, o:o + 1], [[TAPS, 32]]),
                                 ones[0:1, 0:1], start=True, stop=True)
            ins.then_inc(setup_ps, 1)
            pe.wait_ge(ones_set, 3)
            for h in range(2):
                ins = nc.tensor.transpose(acc_ps[:, 0, h * 128:(h + 1) * 128], w1_ordered[:, h * 128:(h + 1) * 128], ident[:, :])
            ins.then_inc(setup_ps, 1)
            group_mean(0)
            pe.wait_ge(setup_sb, 9)
            for k in range(NK):
                make_t(0, k)
            pe.wait_ge(abs_sum, 1)
            mm(sb_ps[:, 64:65], ones[:, :], cf[:, 24:25], start=True, stop=True).then_inc(abs_ps, 1)
            pe.wait_ge(wq_ready, 1)
            pe.wait_ge(ones_set, 2)
            for r in range(5):
                if counts(r - 3):
                    pe.wait_ge(wq_sb, r - 3)
                for n in range(8 if r < 4 else 4):
                    o = (r * 8 + n) * 128
                    src = wq_ordered[:, o:o + 128]
                    ins = nc.tensor.transpose(wt_ps[:, r % 4, :].bitcast(bf16)[:, n * 128:(n + 1) * 128], src, ident_b)
                ins.then_inc(wq_ps, 1)
            pe.wait_ge(wq_sb, 5)
            for kind, n in ORDER[:5]:
                make(0, 0, kind, n)
            image(0, True, False)
            with pe.Fori(1, B - 1) as b:
                image(b, False, False)
            image(B - 1, False, True)

            NI = 2 * B
            small = raw[:, 1, 1, :]
            pe.wait_ge(gsum_in, 1)
            mm(misc_ps[:, 0:2 * NI], mask[:, :], raw[:, 0, 0, 64:64 + 2 * NI], start=True, stop=True).then_inc(gsum_ps, 1)
            pe.wait_ge(gsum_in, 3)
            mm(misc_ps[:, 64:64 + 2 * B], ones[:, :], raw[:, 0, 1, 12 * NI:13 * NI], start=True, stop=True).then_inc(gsum_ps, 1)
            pe.wait_ge(gsum_in, 5)
            pe.wait_ge(ident_in, 16)
            mm(misc_ps[0:1, 128:256], small[:, 16:17], ident2, start=True, stop=True).then_inc(gsum_ps, 1)
            pe.wait_ge(gsum_in, 6)
            mm(misc_ps[:, 256:257], ones[0:1, :], small[0:1, 18:19], start=True, stop=True).then_inc(gsum_ps, 1)

            def conv(b, par):
                pe.wait_ge(q_ready, (b + 1) * 4)
                for n in range(TILES):
                    k, m = divmod(n, 2)
                    slot = (TILES * par + n) % 4
                    if counts(b * TILES + n - 3):
                        pe.wait_ge(y_scaled, b * TILES + n - 3)
                    c = 0
                    for kh in range(2):
                        src = xq(par)[:, kh, :].rearrange("p (r c) -> p r c", c=CW)
                        for tap in range(KK):
                            dy, dx = divmod(tap, 3)
                            o = ((m * 2 + kh) * KK + tap) * 128
                            ins = mm(conv_bank(slot), wqT[:, o:o + 128], src[:, ROWS * k + dy:ROWS * k + dy + ROWS, dx:dx + HW],
                                     start=c == 0, stop=c == 2 * KK - 1)
                            c += 1
                    ins.then_inc(conv_done, 1)

            pe.wait_ge(wq_in, 16)
            for par in range(2):
                conv(par, par)
            with pe.Fori(1, B // 2) as j:
                for par in range(2):
                    conv(j * 2 + par, par)


_INS = ["x", "L0_conv_w1", "L0_conv_b1", "L0_conv_w2", "L0_conv_b2", "L1_conv_weight", "L1_conv_bias",
        "L1_conv_ln_weight", "L1_conv_ln_bias"]


def kernel(**inputs):
    import numpy as _np
    import concourse.bacc as _bacc
    from concourse import mybir as _mybir
    from concourse.bass_utils import run_bass_kernel_spmd as _run

    nc = _bacc.Bacc("TRN2", target_bir_lowering=False, num_devices=1)
    part = _np.arange(128)
    shapes = {
        "ident": _np.eye(128, dtype=_np.float32),
        "sel": (part[:, None] % 32 == _np.arange(32)[None, :]).astype(_np.float32),
        "mask": ((part[:, None] % 32) // 2 == (part[None, :] % 32) // 2).astype(_np.float32) / 8,
    }
    arrays, args = {}, []
    for name, a in [(n, inputs[n]) for n in _INS] + list(shapes.items()):
        a = _np.ascontiguousarray(a)
        arrays[f"in_{name}"] = a
        args.append(nc.dram_tensor(f"in_{name}", a.shape, _mybir.dt.from_np(a.dtype), kind="ExternalInput").ap())
    args.append(nc.dram_tensor("out_y", (B, C, HW, HW), _mybir.dt.float32, kind="ExternalOutput").ap())
    build(nc, *args)
    r = _run(nc, [arrays], core_ids=[0])
    return r.results[0]["out_y"]
```

```python
from contextlib import ExitStack

import numpy as np

import concourse.bass as bass
from concourse import mybir

B, C, HW = 8, 256, 56
PIX = HW * HW
RC = 128
K, PAD = 7, 3
TAPS = K * K
PW = HW + 2 * PAD
PN = PW * PW
ROWS = 8
NK = HW // ROWS
PX = ROWS * HW
PCH = ROWS * PW
STEPS = 2 * NK
VROWS = PW - 3
HLEN = PN - 3
G = C // 4
GN_EPS = 1e-5
Q_B = 128.0
MAGIC = 1.5 * 2.0 ** 23
CW = HW + 2
CN = CW * CW
KK = 9
TILES = 2 * NK

QUADS = ([("H", r, 0) for r in (0, 1, 2)] + [("V", 0, c) for c in (4, 5, 6)]
         + [("H", r, 3) for r in (4, 5, 6)] + [("V", 3, c) for c in (0, 1, 2)])
CENTRE = 12
DQ = [0, 1, 3, 4, 6, 7, 9, 10]
PQ = [2, 5, 8, 11]
ND, NP = len(DQ), len(PQ)
NS = NP + 1
DRING, PRING = 4, 2
PAIR = (5, 6)
ADDED = [n for n in range(ND) if n not in PAIR]
NA = len(ADDED) + 1


def quad_taps(q):
    if q == CENTRE:
        return [PAD * K + PAD] * 4
    kind, r, c = QUADS[q]
    return [(r * K + c + s) if kind == "H" else ((r + s) * K + c) for s in range(4)]


def build(nc, x, w1, b1, w2, b2, cw, cbias, lnw, lnb, ident_d, sel_d, mask_d, out):
    f32 = mybir.dt.float32
    bf16 = mybir.dt.bfloat16
    ALU = mybir.AluOpType
    ACT = mybir.ActivationFunctionType
    AX = mybir.AxisListType.X

    xs = x.rearrange("b (h g s) r w -> b h s g (r w)", h=2, s=4)
    outs = out.rearrange("b (h g s) r w -> b h s g (r w)", h=2, s=4)
    xn_d = nc.dram_tensor("xn_padded", (B, C, PN), f32).ap()
    xns = xn_d.rearrange("b (h g s) n -> b h s g n", h=2, s=4)
    t_d = nc.dram_tensor("t_all", (B, RC, PIX), f32).ap()
    x1_d = nc.dram_tensor("x1_all", (B, 2, 128, PIX), f32).ap()
    wq_d = nc.dram_tensor("wq_all", (128, 4 * KK * 128), bf16).ap()

    nc.disable_value_cache = True
    ctx = ExitStack()
    with ctx:
        def sb(name, shape, dt=f32):
            return ctx.enter_context(nc.sbuf_tensor(name, shape, dt))

        def ps(name, shape):
            return ctx.enter_context(nc.psum_tensor(name, shape, f32))

        def sem(name):
            return ctx.enter_context(nc.semaphore(name))

        def counts(value):
            return not isinstance(value, int) or value > 0

        def view(ap, dims):
            return bass.AP(ap.tensor, ap.offset, [list(ap.ap[0])] + dims)

        shift_rows = sb("shift_rows", [128, 4, VROWS * PW])
        shift_cols = sb("shift_cols", [128, 4, HLEN])
        prod = sb("prod", [128, DRING + PRING, 4 * PX])
        w2T = sb("w2T", [128, 2, 13, 128])
        w1T = sb("w1T", [128, 2, 128])
        wt_sb = sb("wt_sb", [128, 2, PX])
        t_in = sb("t_in", [128, 2, PX])
        xres = sb("xres", [128, 2, PX])
        xc = sb("xc", [128, 2, PCH])
        raw = sb("raw", [128, 2, 2, PX])
        xn = sb("xn", [128, 2, PCH])
        t_out = sb("t_out", [128, PX])
        mask = sb("mask", [128, 128])
        ones = sb("ones", [128, 128])
        sel = sb("sel", [128, 32])
        b2c = sb("b2c", [128, 26])
        cols = sb("cols", [128, 8])
        b1c, lnw_c, lnb_c, bias_c = cols[:, 0:1], cols[:, 1:3], cols[:, 3:5], cols[:, 5:7]
        sums = sb("sums", [128, 4, NK])
        cf = sb("cf", [128, 32])
        st_image = sb("st_image", [128, 4, STEPS])
        st_all = sb("st_all", [128, 4, B, STEPS])
        junk = sb("junk", [128, PX])
        junk2 = sb("junk2", [128, PX])

        H = shift_cols[:, :, :].rearrange("p a b -> p (a b)")
        V = shift_rows[:, :, :].rearrange("p a b -> p (a b)")
        P = prod[:, :, :].rearrange("p a b -> p (a b)")
        w2_raw = H[0:G, 0:TAPS * 128]
        b2_row = H[0:1, 6272:6272 + TAPS * G]
        w1_raw = H[:, 9408:9408 + C]
        w1_ordered = H[:, 9664:9664 + C]
        ident = P[:, 9216:9344]
        ident_b = P[:, 9344:9408].bitcast(bf16)
        zeros = V[:, 0:16 * PAD * PW]
        x_first = V[:, 3000:3000 + 2 * PIX].rearrange("p (h n) -> p h n", h=2)
        square_out = V[:, 9300:9300 + PIX]
        xn_first = [H[:, 9920 + n * 2 * PCH:9920 + (n + 1) * 2 * PCH].rearrange("p (h n) -> p h n", h=2) for n in range(4)]
        t_first = [H[:, 13888 + n * PX:13888 + (n + 1) * PX] for n in range(3)]
        cw_raw = P[:, 0:2 * C * KK]
        wq = P[:, 4608:6912].bitcast(bf16)
        wneg = P[:, 6912:9216].bitcast(bf16)
        wq_ordered = P[:, 0:2304].bitcast(bf16)
        wqT_stage = wneg

        wt_ps = ps("wt_ps", [128, DRING, 512])
        sb_ps = ps("sb_ps", [128, 512])
        acc_ps = ps("acc_ps", [128, 2, 512])
        misc_ps = ps("misc_ps", [128, 512])

        const_in = sem("const_in")
        vec_in = sem("vec_in")
        w2_in = sem("w2_in")
        x_first_in = sem("x_first_in")
        squares_done = sem("squares_done")
        xn_first_stored = [sem(f"xn_first_stored{n}") for n in range(4)]
        t_first_stored = [sem(f"t_first_stored{n}") for n in range(3)]
        cw_in = sem("cw_in")
        zero_set = sem("zero_set")
        sums_zero = sem("sums_zero")
        squares_one = sem("squares_one")
        zero_stored = sem("zero_stored")
        ones_set = sem("ones_set")
        setup_ps = sem("setup_ps")
        setup_sb = sem("setup_sb")
        abs_sum = sem("abs_sum")
        abs_ps = sem("abs_ps")
        wq_ready = sem("wq_ready")
        wq_ps = sem("wq_ps")
        wq_sb = sem("wq_sb")
        wq_stored = sem("wq_stored")
        chain0 = sem("chain0")
        chain1 = sem("chain1")
        raw_in = [sem(f"raw_in{p}") for p in range(2)]
        stat_done = sem("stat_done")
        coef_in = sem("coef_in")
        coef_ps = sem("coef_ps")
        var_ready = sem("var_ready")
        std_ready = sem("std_ready")
        coef_done = sem("coef_done")
        norm_done = sem("norm_done")
        t_ps = sem("t_ps")
        t_ready = sem("t_ready")
        xn_stored = sem("xn_stored")
        t_stored = sem("t_stored")
        tin_in = [sem(f"tin_in{p}") for p in range(2)]
        xc_in = [sem(f"xc_in{p}") for p in range(2)]
        xres_in = [sem(f"xres_in{p}") for p in range(2)]
        shift_in = [sem(f"shift_in{k}") for k in range(NK)]
        d_made = sem("d_made")
        s_made = sem("s_made")
        d_biased = sem("d_biased")
        s_biased = sem("s_biased")
        d_mult = sem("d_mult")
        centre_mult = sem("centre_mult")
        s_used = sem("s_used")
        pair_sum = sem("pair_sum")
        d_added = sem("d_added")
        p_added = sem("p_added")
        x1_ready = sem("x1_ready")
        x1_min = sem("x1_min")
        x1_sums = sem("x1_sums")
        x1_kept = sem("x1_kept")
        sums_kept = sem("sums_kept")
        x1_stored = sem("x1_stored")
        gsum_in = sem("gsum_in")
        gsum_ps = sem("gsum_ps")
        gstd = sem("gstd")
        affine_ready = sem("affine_ready")
        border_set = sem("border_set")
        wq_in = sem("wq_in")
        x1_in = [sem(f"x1_in{p}") for p in range(2)]
        ident_in = sem("ident_in")
        shown_ready = sem("shown_ready")
        act_q = sem("act_q")
        q_ready = sem("q_ready")
        conv_done = sem("conv_done")
        y_scaled = sem("y_scaled")
        y_ready = sem("y_ready")
        y_stored = [sem(f"y_stored{p}") for p in range(4)]

        def linker(eng, s, base):
            n = [0]

            def link(ins):
                n[0] += 1
                ins.then_inc(s, 1)
                eng.wait_ge(s, base + n[0])
            return link

        def shifted(q, k):
            kind, r, c = QUADS[q]
            buf, pitch = (shift_cols, HLEN) if kind == "H" else (shift_rows, VROWS * PW)
            a = buf[:, 0, (ROWS * k + r) * PW + c:(ROWS * k + r) * PW + c + 1]
            return view(a, [[pitch, 4], [PW, ROWS], [1, HW]])

        def broadcast(wt):
            return view(wt, [[0, 4], [HW, ROWS], [1, HW]])

        def product(n):
            return view(prod[:, n % DRING, 0:1], [[PX, 4], [HW, ROWS], [1, HW]])

        def pool_product(n):
            return view(prod[:, DRING + n % PRING, 0:1], [[PX, 4], [HW, ROWS], [1, HW]])

        ORDER = [("D", 0), ("D", 1), ("S", 0), ("D", 2), ("S", 1), ("D", 3), ("S", 2), ("D", 4), ("D", 5), ("S", 3),
                 ("D", 6), ("D", 7), ("S", 4)]
        AHEAD = 6

        def first_bank(k):
            return misc_ps[:, 0:PX] if k % 2 == 0 else acc_ps[:, 1, 0:PX]

        def quad_of(kind, n):
            return DQ[n] if kind == "D" else (PQ[n - 1] if n else CENTRE)

        def x1b(par):
            return V[:, par * 2 * PIX:(par + 1) * 2 * PIX].rearrange("p (h n) -> p h n", h=2)

        XQ = CN
        def xq(par):
            return H[:, par * XQ:(par + 1) * XQ].bitcast(bf16).rearrange("p (h n) -> p h n", h=2)

        HALF = PIX // 2
        def qtmp(q):
            return H[:, 2 * XQ + (q % 2) * HALF:2 * XQ + (q % 2 + 1) * HALF]

        wqT = H[:, 2 * XQ + 2 * HALF:2 * XQ + 2 * HALF + 2 * KK * 128].bitcast(bf16)

        ident2 = xc[:, 0, 0:128]

        def ybuf(slot):
            return prod[:, slot, 0:PX]

        def conv_bank(t):
            return wt_ps[:, t, 0:PX]

        block = ctx.enter_context(nc.Block())

        @block.sync
        def _(sp):
            def load_raw(b, j):
                if 2 <= j < NK + 2:
                    sp.wait_ge(stat_done, (b - 1) * NK + (j - 2) + 1)
                else:
                    sp.wait_ge(norm_done, b * NK + (j - 2 - NK if j >= 2 else j - 2) + 1)
                k = j % NK
                for h in range(2):
                    sp.dma_start(raw[:, j % 2, h, :], xs[b, h, :, :, k * PX:(k + 1) * PX]).then_inc(raw_in[j % 2], 16)

            def store_norm(b, k):
                sp.wait_ge(norm_done, b * NK + k + 1)
                o = (ROWS * k + PAD) * PW
                for h in range(2):
                    sp.dma_start(xns[b, h, :, :, o:o + PCH], xn[:, h, :]).then_inc(xn_stored, 16)
                sp.wait_ge(t_ready, b * NK + k + 1)
                sp.dma_start(t_d[b, :, k * PX:(k + 1) * PX], t_out[:, :]).then_inc(t_stored, 16)

            def store_first(k):
                sp.wait_ge(norm_done, k + 1)
                o = (ROWS * k + PAD) * PW
                for h in range(2):
                    sp.dma_start(xns[0, h, :, :, o:o + PCH], xn_first[k % 4][:, h, :]).then_inc(xn_first_stored[k % 4], 16)
                sp.wait_ge(t_ready, k + 1)
                sp.dma_start(t_d[0, :, k * PX:(k + 1) * PX], t_first[k % 3]).then_inc(t_first_stored[k % 3], 16)

            def wait_norm_stored(b, k):
                if isinstance(b, int) and b == 0:
                    sp.wait_ge(xn_first_stored[k % 4], (k // 4 + 1) * 32)
                else:
                    sp.wait_ge(xn_stored, ((b - 1) * NK + k + 1) * 32)

            def wait_t_stored(b, k):
                if isinstance(b, int) and b == 0:
                    sp.wait_ge(t_first_stored[k % 3], (k // 3 + 1) * 16)
                else:
                    sp.wait_ge(t_stored, ((b - 1) * NK + k + 1) * 16)

            def load_shifted(b, h, k):
                wait_norm_stored(b, k)
                o = k * PCH
                nv = PCH if k < NK - 1 else VROWS * PW - o
                nh = PCH if k < NK - 1 else HLEN - o
                src = xn_d[b, h * 128:(h + 1) * 128, :]
                for s in range(4):
                    p = slice(32 * s, 32 * s + 32)
                    for dst, n, d in ((shift_rows, nv, s * PW), (shift_cols, nh, s)):
                        sp.dma_start(dst[p, :, o:o + n], src[:, o + d:o + d + n].rearrange("(g q) n -> g q n", q=4)
                                     ).then_inc(shift_in[k], 16)

            def load_step(b, i):
                h, k = divmod(i, NK)
                wait_t_stored(b, k)
                sp.dma_start(t_in[:, i % 2, :], t_d[b, :, k * PX:(k + 1) * PX]).then_inc(tin_in[i % 2], 16)
                wait_norm_stored(b, k)
                o = (ROWS * k + PAD) * PW
                sp.dma_start(xc[:, i % 2, :], xns[b, h, :, :, o:o + PCH]).then_inc(xc_in[i % 2], 16)

            def load_xres(b, i):
                h, k = divmod(i, NK)
                sp.dma_start(xres[:, i % 2, :], xs[b, h, :, :, k * PX:(k + 1) * PX]).then_inc(xres_in[i % 2], 16)

            def store_x1(b, i):
                h, k = divmod(i, NK)
                s = b * STEPS + i
                sp.wait_ge(x1_ready, s + 1)
                sp.dma_start(x1_d[b, h, :, k * PX:(k + 1) * PX], xres[:, i % 2, :]).then_inc(x1_stored, 16)

            def image(b, first, last):
                for i in range(STEPS):
                    s = b * STEPS + i
                    if not last:
                        load_raw(b + 1, i)
                    if counts(s * ND):
                        sp.wait_ge(d_mult, s * ND)
                    if counts(s * NS):
                        sp.wait_ge(s_used, s * NS)
                    if not (last and i == STEPS - 1):
                        load_step(*((b, i + 1) if i + 1 < STEPS else (b + 1, 0)))
                    if first and i + 2 < NK:
                        load_shifted(0, 0, i + 2)
                    if i == 0 and not first:
                        load_shifted(b, 0, NK - 1)
                    elif 1 <= i <= NK:
                        load_shifted(b, 1, i - 1)
                    elif i > NK and not last:
                        load_shifted(b + 1, 0, i - NK - 1)
                    if not (first and i == 0):
                        store_x1(*((b, i - 1) if i else (b - 1, STEPS - 1)))
                    if not (last and i == STEPS - 1):
                        if counts(s):
                            sp.wait_ge(x1_sums, s)
                        if counts(s * 16):
                            sp.wait_ge(x1_stored, s * 16)
                        load_xres(*((b, i + 1) if i + 1 < STEPS else (b + 1, 0)))
                    if i >= NK and not last:
                        store_norm(b + 1, i - NK)

            for h in range(2):
                sp.dma_start(x_first[:, h, :], xs[0, h, :, :, :]).then_inc(x_first_in, 16)
            for dst, src in ((sel[:, :], sel_d), (mask[:, :], mask_d), (ident, ident_d), (w1_raw, w1),
                             (b1c, b1.rearrange("(p o) -> p o", o=1))):
                sp.dma_start(dst, src).then_inc(const_in, 16)
            sp.dma_start(w2_raw.rearrange("g (p r) -> g p r", r=128), w2.rearrange("(g p) r -> g p r", p=TAPS)).then_inc(w2_in, 16)
            sp.dma_start(b2_row, b2.rearrange("(a n) -> a n", a=1)).then_inc(w2_in, 16)
            for dst, src in ((lnw_c, lnw), (lnb_c, lnb), (bias_c, cbias)):
                v = src.rearrange("(h g s o) -> h s g o", h=2, s=4, o=1)
                for h in range(2):
                    sp.dma_start(dst[:, h:h + 1], v[h], allow_slow_non_contiguous=True).then_inc(vec_in, 16)
            sp.wait_ge(zero_set, 1)
            allrows = xn_d.rearrange("b c n -> (b c) n").rearrange("(p q) n -> p q n", q=16)
            for o in (0, PN - PAD * PW):
                sp.dma_start(allrows[:, :, o:o + PAD * PW], zeros.rearrange("p (q n) -> p q n", q=16)).then_inc(zero_stored, 16)
            cws = cw.rearrange("(m g s) i a b -> m s g (i a b)", m=2, s=4)
            for m in range(2):
                sp.dma_start(cw_raw[:, m * C * KK:(m + 1) * C * KK], cws[m]).then_inc(cw_in, 16)
            for k in range(NK):
                store_first(k)
            for n in range(4):
                sp.wait_ge(xn_first_stored[n], len(range(n, NK, 4)) * 32)
            for n in range(3):
                sp.wait_ge(t_first_stored[n], len(range(n, NK, 3)) * 16)
            sp.wait_ge(zero_stored, 32)
            sp.wait_ge(setup_sb, 9)
            for k in range(2):
                load_shifted(0, 0, k)
            load_step(0, 0)
            load_xres(0, 0)
            image(0, True, False)
            with sp.Fori(1, B - 1) as b:
                image(b, False, False)
            image(B - 1, False, True)
            store_x1(B - 1, STEPS - 1)

            def load_x1(b, par):
                for h in range(2):
                    sp.dma_start(x1b(par)[:, h, :], x1_d[b, h, :, :]).then_inc(x1_in[par], 16)

            sp.wait_ge(d_mult, B * STEPS * ND)
            sp.wait_ge(s_used, B * STEPS * NS)
            sp.wait_ge(x1_stored, B * STEPS * 16)
            sp.wait_ge(wq_stored, 16)
            sp.dma_start(ident2, ident_d).then_inc(ident_in, 16)
            load_x1(0, 0)
            sp.dma_start(wqT, wq_d).then_inc(wq_in, 16)
            load_x1(1, 1)

            def stores(b, par, more):
                for n in range(TILES):
                    k, m = divmod(n, 2)
                    slot = (TILES * par + n) % 4
                    sp.wait_ge(y_ready, b * TILES + n + 1)
                    sp.dma_start(outs[b, m, :, :, k * PX:(k + 1) * PX], ybuf(slot)).then_inc(y_stored[slot], 16)
                if more:
                    load_x1(b + 2, par)

            for par in range(2):
                stores(par, par, True)
            with sp.Fori(1, B // 2 - 1) as j:
                for par in range(2):
                    stores(j * 2 + par, par, True)
            for par in range(2):
                stores(B - 2 + par, par, False)
            for slot in range(4):
                sp.wait_ge(y_stored[slot], B * TILES // 4 * 16)

        @block.vector
        def _(dve):
            v = nc.vector
            NL0 = 10

            def coef_a(b):
                dve.wait_ge(stat_done, b * NK)
                v.tensor_reduce(cf[:, 0:4], sums[:, :, :], AX, ALU.add).then_inc(coef_in, 1)

            def coef_b(b):
                link = linker(dve, chain0, b * NL0)
                dve.wait_ge(coef_ps, b + 1)
                link(v.tensor_scalar_mul(cf[:, 4:8], misc_ps[:, 0:4], 1.0 / PIX))
                link(v.tensor_tensor(cf[:, 16:18], cf[:, 4:6], cf[:, 4:6], ALU.mult))
                link(v.tensor_tensor(cf[:, 18:20], cf[:, 6:8], cf[:, 16:18], ALU.subtract))
                v.tensor_scalar_add(cf[:, 8:10], cf[:, 18:20], GN_EPS).then_inc(var_ready, 1)

            def newton(link, var, root, inv, tmp, last):
                link(v.reciprocal(inv, root))
                link(v.tensor_tensor(tmp, inv, inv, ALU.mult))
                link(v.tensor_tensor(tmp, tmp, var, ALU.mult))
                link(v.tensor_scalar(tmp, tmp, -0.5, 1.5, ALU.mult, ALU.add))
                last(v.tensor_tensor(inv, inv, tmp, ALU.mult))

            def coef_c(b):
                link = linker(dve, chain0, b * NL0 + 3)
                dve.wait_ge(std_ready, b + 1)
                if counts(b * NK):
                    dve.wait_ge(norm_done, b * NK)
                newton(link, cf[:, 8:10], cf[:, 10:12], cf[:, 12:14], cf[:, 16:18], link)
                link(v.tensor_tensor(cf[:, 18:20], cf[:, 4:6], cf[:, 12:14], ALU.mult))
                link(v.tensor_scalar_mul(cf[:, 14:16], cf[:, 18:20], -1.0))
                v.nop().then_inc(coef_done, 1)

            def finish(b, i):
                s = b * STEPS + i
                if i == 0 and counts(b):
                    dve.wait_ge(x1_kept, b)
                dve.wait_ge(d_added, (s + 1) * NA)
                dve.wait_ge(p_added, (s + 1) * NP)
                dve.wait_ge(s_used, s * NS + 1)
                v.memset(cf[:, 30:31], 0.0)
                v.tensor_tensor_reduce(out=xres[:, i % 2, :], in0=acc_ps[:, i % 2, 0:PX], in1=xres[:, i % 2, :], scale=1.0,
                                       scalar=-3.0e38, op0=ALU.add, op1=ALU.max, accum_out=st_image[:, 2, i:i + 1]).then_inc(x1_ready, 1)
                dve.wait_ge(x1_ready, s + 1)
                v.tensor_reduce(st_image[:, 3, i:i + 1], xres[:, i % 2, :], AX, ALU.min).then_inc(x1_min, 1)

            def keep_stats(b):
                dve.wait_ge(x1_min, (b + 1) * STEPS)
                one = slice(b, b + 1) if isinstance(b, int) else bass.ds(b, 1)
                v.tensor_copy(st_all[:, 2:4, one, :].rearrange("p t b n -> p t (b n)"), st_image[:, 2:4, :]).then_inc(x1_kept, 1)

            def image(b, first, last):
                for i in range(STEPS):
                    k = i % NK
                    s = b * STEPS + i
                    phase = b * 2 + i // NK
                    for n in range(ND):
                        if n == 0:
                            for kk in (k, k + 1)[:2 if k + 1 < NK else 1]:
                                dve.wait_ge(shift_in[kk], (phase + 1) * 128)
                        dve.wait_ge(d_biased, s * ND + n + 1)
                        if n < DRING and n % DRING != PAIR[0] % DRING:
                            before = (s - 1) * NA + (ADDED + [PAIR[1]]).index(n + DRING) + 1
                            if counts(before):
                                dve.wait_ge(d_added, before)
                        elif n < DRING:
                            if counts(s):
                                dve.wait_ge(pair_sum, s)
                        else:
                            dve.wait_ge(d_added, s * NA + n - DRING + 1)
                        v.tensor_tensor(product(n), broadcast(wt_ps[:, n % DRING, 0:PX]), shifted(DQ[n], k), ALU.mult
                                        ).then_inc(d_mult, 1)
                        if n == 1 and i == NK and not last:
                            coef_c(b + 1)
                        if n == 1 and not (first and i == 0):
                            finish(*((b, i - 1) if i else (b - 1, STEPS - 1)))
                        if n == 2 and i == 0 and not first:
                            keep_stats(b - 1)
                        if n == 4 and i == NK - 1 and not last:
                            coef_a(b + 1)
                    dve.wait_ge(d_mult, s * ND + PAIR[1] + 1)
                    two = [prod[:, n % DRING, :] for n in PAIR]
                    v.tensor_tensor(two[1], two[0], two[1], ALU.add).then_inc(pair_sum, 1)
                    if i == NK - 1 and not last:
                        coef_b(b + 1)

            v.memset(sums[:, :, :], 0.0).then_inc(sums_zero, 1)
            dve.wait_ge(sums_zero, 1)
            dve.wait_ge(x_first_in, 32)
            for h in range(2):
                ins = v.tensor_reduce(sums[:, h, 0:1], x_first[:, h, :], AX, ALU.add)
            ins.then_inc(squares_done, 1)
            dve.wait_ge(squares_done, 2)
            v.tensor_reduce(cf[:, 0:4], sums[:, :, :], AX, ALU.add).then_inc(coef_in, 1)
            coef_b(0)
            coef_c(0)
            dve.wait_ge(const_in, 80)
            dve.wait_ge(ones_set, 1)
            v.tensor_copy(ident_b, ident).then_inc(ones_set, 1)
            for h in range(2):
                last_copy = v.tensor_copy(view(w1_ordered[:, h * 128:h * 128 + 1], [[32, 4], [1, 32]]),
                                          view(w1_raw[:, h * 128:h * 128 + 1], [[1, 4], [4, 32]]))
            last_copy.then_inc(ones_set, 1)
            where = {t: [(q, s) for q in range(13) for s, u in enumerate(quad_taps(q)) if u == t] for t in range(TAPS)}
            for r in range(K):
                dve.wait_ge(setup_ps, r + 1)
                for c in range(K):
                    src = wt_ps[:, r % 4, c * G:(c + 1) * G].rearrange("p (h g) -> p h g", h=2)
                    for q, s in where[r * K + c]:
                        last_copy = v.tensor_copy(w2T[:, :, q, 32 * s:32 * s + 32], src)
                last_copy.then_inc(setup_sb, 1)
            dve.wait_ge(setup_ps, 8)
            v.tensor_copy(b2c[:, :], sb_ps[:, 0:26]).then_inc(setup_sb, 1)
            dve.wait_ge(setup_ps, 9)
            v.tensor_copy(w1T[:, :, :].rearrange("p a b -> p (a b)"), acc_ps[:, 0, 0:256]).then_inc(setup_sb, 1)
            dve.wait_ge(cw_in, 32)
            v.tensor_reduce(cf[:, 24:25], cw_raw, AX, ALU.add, apply_absolute_value=True).then_inc(abs_sum, 1)
            dve.wait_ge(abs_ps, 1)
            wl = linker(dve, chain1, 0)
            wl(v.tensor_scalar(cf[:, 25:26], sb_ps[:, 64:65], 1.0 / (C * C * KK), 0.7, ALU.mult, ALU.mult))
            wl(v.tensor_scalar_mul(cf[:, 26:27], cf[:, 25:26], -1.0))
            wl(v.tensor_scalar(wq, cw_raw, cf[:, 25:26], None, ALU.is_gt))
            wl(v.tensor_scalar(wneg, cw_raw, cf[:, 26:27], None, ALU.is_lt))
            for mk in range(4):
                o = mk * KK * 128
                src = [view(a[:, o:o + 1], [[KK, 4], [4 * KK, 32], [1, KK]]) for a in (wq, wneg)]
                ins = v.tensor_tensor(view(wq_ordered[:, o:o + 1], [[32, 4], [1, 32], [128, KK]]), src[0], src[1], ALU.subtract)
            ins.then_inc(wq_ready, 1)
            dve.wait_ge(wq_stored, 16)

            image(0, True, False)
            with dve.Fori(1, B - 1) as b:
                image(b, False, False)
            image(B - 1, False, True)
            finish(B - 1, STEPS - 1)
            keep_stats(B - 1)

            dve.wait_ge(vec_in, 96)
            link = linker(dve, chain1, 4)
            NI = 2 * B
            g2 = raw[:, 0, 0, 64:64 + 2 * NI]
            w = [raw[:, 0, 1, NI * n:NI * (n + 1)] for n in range(24)]
            gm, gv, root, rg, tmp, dd, e1, e2, aa, bb, mxr, mnr = w[:12]
            var_c = w[15]
            us, uu = w[12], w[13]
            cand = raw[:, 1, 0, 0:2 * NI]
            small = raw[:, 1, 1, :]
            by_half = st_all[:, :, :, :].rearrange("p t b (h k) -> p t (b h) k", h=2)
            dve.wait_ge(x1_kept, B)
            link(v.tensor_reduce(mxr, by_half[:, 2], AX, ALU.max))
            link(v.tensor_reduce(mnr, by_half[:, 3], AX, ALU.min))
            dve.wait_ge(sums_kept, B)
            link(v.tensor_reduce(g2, by_half[:, 0:2].rearrange("p t n k -> p (t n) k"), AX, ALU.add))
            link(v.tensor_scalar_mul(g2, g2, 1.0 / PIX))
            v.nop().then_inc(gsum_in, 1)
            dve.wait_ge(gsum_ps, 1)
            link(v.tensor_copy(gm, misc_ps[:, 0:NI]))
            link(v.tensor_tensor(tmp, gm, gm, ALU.mult))
            link(v.tensor_tensor(gv, misc_ps[:, NI:2 * NI], tmp, ALU.subtract))
            link(v.tensor_scalar_add(gv, gv, GN_EPS))
            v.nop().then_inc(gsum_in, 1)
            dve.wait_ge(gstd, 1)
            newton(link, gv, root, rg, tmp, link)
            link(v.tensor_tensor(tmp, g2[:, 0:NI], g2[:, 0:NI], ALU.mult))
            link(v.tensor_tensor(var_c, g2[:, NI:2 * NI], tmp, ALU.subtract))
            link(v.tensor_tensor(dd, g2[:, 0:NI], gm, ALU.subtract))
            link(v.tensor_tensor(e1, dd, rg, ALU.mult))
            link(v.tensor_tensor(e2, dd, dd, ALU.mult))
            link(v.tensor_tensor(e2, e2, var_c, ALU.add))
            link(v.tensor_tensor(e2, e2, rg, ALU.mult))
            link(v.tensor_tensor(e2, e2, rg, ALU.mult))
            link(v.tensor_tensor(us[:, 0:B], e1[:, 0:NI:2], e1[:, 1:NI:2], ALU.add))
            link(v.tensor_tensor(us[:, B:2 * B], e2[:, 0:NI:2], e2[:, 1:NI:2], ALU.add))
            v.nop().then_inc(gsum_in, 1)
            dve.wait_ge(gsum_ps, 2)
            link(v.tensor_scalar_mul(uu, misc_ps[:, 64:64 + 2 * B], 1.0 / C))
            mu, v2 = uu[:, 0:B], uu[:, B:2 * B]
            link(v.tensor_tensor(tmp[:, 0:B], mu, mu, ALU.mult))
            link(v.tensor_tensor(v2, v2, tmp[:, 0:B], ALU.subtract))
            link(v.tensor_scalar_add(v2, v2, GN_EPS))
            v.nop().then_inc(gsum_in, 1)
            dve.wait_ge(gstd, 2)
            r2 = w[14][:, 0:B]
            newton(link, v2, small[:, 0:B], r2, tmp[:, 0:B], link)

            def per_image(a):
                return view(a, [[1, B], [0, 2]])

            def per_half(a):
                return view(a, [[0, B], [1, 2]])

            def three(a):
                return view(a, [[2, B], [1, 2]])

            link(v.tensor_tensor(three(aa), three(rg), per_image(r2), ALU.mult))
            link(v.tensor_tensor(three(aa), three(aa), per_half(lnw_c), ALU.mult))
            link(v.tensor_tensor(tmp, gm, rg, ALU.mult))
            link(v.tensor_tensor(three(tmp), three(tmp), per_image(mu), ALU.add))
            link(v.tensor_tensor(three(tmp), three(tmp), per_image(r2), ALU.mult))
            link(v.tensor_tensor(three(tmp), three(tmp), per_half(lnw_c), ALU.mult))
            link(v.tensor_tensor(three(bb), per_half(lnb_c), three(tmp), ALU.subtract))
            for n, ext in enumerate((mxr, mnr)):
                c = cand[:, n * NI:(n + 1) * NI]
                link(v.tensor_tensor(c, aa, ext, ALU.mult))
                link(v.tensor_tensor(c, c, bb, ALU.add))
            link(v.tensor_reduce(small[:, 16:17], cand, AX, ALU.max, apply_absolute_value=True))
            v.nop().then_inc(gsum_in, 1)
            dve.wait_ge(gsum_ps, 3)
            link(v.tensor_reduce(small[0:1, 17:18], misc_ps[0:1, 128:256], AX, ALU.max))
            link(v.tensor_scalar_max(small[0:1, 18:19], small[0:1, 17:18], 1e-6))
            v.nop().then_inc(gsum_in, 1)
            dve.wait_ge(gsum_ps, 4)
            gam, rq, ys = small[:, 19:20], small[:, 20:21], small[:, 21:22]
            link(v.tensor_copy(gam, misc_ps[:, 256:257]))
            link(v.reciprocal(rq, gam))
            link(v.tensor_scalar_mul(rq, rq, Q_B))
            link(v.tensor_scalar(ys, gam, 1.0 / Q_B, 0.01, ALU.mult, ALU.mult))
            link(v.tensor_scalar(aa, aa, rq, None, ALU.mult))
            link(v.tensor_scalar(bb, bb, rq, None, ALU.mult))
            v.nop().then_inc(affine_ready, 1)
            NQ = 8
            def quantise(b, q, par):
                half, h = divmod(q, 2)
                lq = linker(dve, chain0, B * NL0 + b * NQ + 2 * q)
                dve.wait_ge(act_q, b * 4 + q + 1)
                if q == 0:
                    if counts((b - 1) * TILES):
                        dve.wait_ge(conv_done, (b - 1) * TILES)
                lq(v.tensor_scalar(qtmp(q), qtmp(q), MAGIC, MAGIC, ALU.add, ALU.subtract))
                inner = xq(par)[:, h, :].rearrange("p (r c) -> p r c", c=CW)[:, 1 + 28 * half:29 + 28 * half, 1:1 + HW]
                lq(v.tensor_scalar(inner, qtmp(q).rearrange("p (r c) -> p r c", c=HW), Q_B, -Q_B, ALU.min, ALU.max))
                v.nop().then_inc(q_ready, 1)

            def outputs(b, par, more):
                for n in range(TILES):
                    k, m = divmod(n, 2)
                    slot = (TILES * par + n) % 4
                    dve.wait_ge(y_scaled, b * TILES + n + 1)
                    v.tensor_tensor(ybuf(slot), ybuf(slot), x1b(par)[:, m, k * PX:(k + 1) * PX], ALU.add).then_inc(y_ready, 1)
                    if more and n in (1, 3, 5, 7):
                        quantise(b + 1, n // 2, 1 - par)

            dve.wait_ge(border_set, 1)
            for q in range(4):
                quantise(0, q, 0)
            for par in range(2):
                outputs(par, par, True)
            with dve.Fori(1, B // 2 - 1) as j:
                for par in range(2):
                    outputs(j * 2 + par, par, True)
            for par in range(2):
                outputs(B - 2 + par, par, par == 0)

        @block.gpsimd
        def _(pool):
            g = nc.gpsimd

            def image(b, first, last):
                for i in range(STEPS):
                    k = i % NK
                    s = b * STEPS + i
                    phase = b * 2 + i // NK
                    par = i % 2
                    wt = wt_sb[:, i % 2, :]
                    pool.wait_ge(s_biased, s * NS + 1)
                    pool.wait_ge(xc_in[par], (b * NK + i // 2 + 1) * 16)
                    rows = lambda a: a.rearrange("p (r c) -> p r c", c=HW)
                    centre = xc[:, par, :].rearrange("p (r c) -> p r c", c=PW)[:, :, PAD:PAD + HW]
                    g.tensor_tensor(rows(wt), rows(wt), centre, ALU.mult).then_inc(centre_mult, 1)
                    pool.wait_ge(centre_mult, s + 1)
                    pool.wait_ge(xres_in[par], (b * NK + i // 2 + 1) * 16)
                    g.tensor_tensor(xres[:, par, :], xres[:, par, :], wt, ALU.add).then_inc(s_used, 1)
                    for kk in (k, k + 1)[:2 if k + 1 < NK else 1]:
                        pool.wait_ge(shift_in[kk], (phase + 1) * 128)
                    for n in range(NP):
                        pool.wait_ge(s_biased, s * NS + n + 2)
                        if counts(s * NP + n + 1 - PRING):
                            pool.wait_ge(p_added, s * NP + n + 1 - PRING)
                        g.tensor_tensor(pool_product(n), broadcast(wt_sb[:, (i + n + 1) % 2, :]), shifted(PQ[n], k), ALU.mult
                                        ).then_inc(s_used, 1)

            g.memset(zeros, 0.0).then_inc(zero_set, 1)
            for n in range(4):
                g.memset(xn_first[n], 0.0)
            g.memset(ones[:, :], 1.0)
            g.memset(xn[:, :, :], 0.0).then_inc(ones_set, 1)
            pool.wait_ge(wq_stored, 16)
            image(0, True, False)
            with pool.Fori(1, B - 1) as b:
                image(b, False, False)
            image(B - 1, False, True)
            pool.wait_ge(d_mult, B * STEPS * ND)
            pool.wait_ge(s_used, B * STEPS * NS)
            for par in range(2):
                ins = g.memset(H[:, par * XQ:(par + 1) * XQ], 0.0)
            ins.then_inc(border_set, 1)

        @block.scalar
        def _(act):
            a = nc.scalar

            def normalise(b, k):
                j = NK + k
                act.wait_ge(coef_done, b + 1)
                act.wait_ge(raw_in[j % 2], ((b - 1) * NK + j // 2 + 1) * 32)
                if counts((b - 1) * NK + k):
                    act.wait_ge(xn_stored, ((b - 1) * NK + k) * 32)
                act.wait_ge(t_ps, b * NK + k)
                for h in range(2):
                    inner = xn[:, h, :].rearrange("p (r c) -> p r c", c=PW)[:, :, PAD:PAD + HW]
                    ins = a.activation(inner, raw[:, j % 2, h, :].rearrange("p (r c) -> p r c", c=HW), ACT.Identity,
                                       bias=cf[:, 14 + h:15 + h], scale=cf[:, 12 + h:13 + h])
                ins.then_inc(norm_done, 1)

            def bias_t(b, k):
                act.wait_ge(t_ps, b * NK + k + 1)
                if counts((b - 1) * NK + k):
                    act.wait_ge(t_stored, ((b - 1) * NK + k) * 16)
                a.activation(t_out[:, :], misc_ps[:, 0:PX], ACT.Identity, bias=b1c).then_inc(t_ready, 1)

            def stats(b, k):
                act.wait_ge(raw_in[k % 2], ((b - 1) * NK + k // 2 + 1) * 32)
                if k == 0:
                    if counts((b - 1) * NK):
                        act.wait_ge(t_stored, (b - 1) * NK * 16)
                if counts((b - 1) * NK + k):
                    act.wait_ge(stat_done, (b - 1) * NK + k)
                for h in range(2):
                    r = raw[:, k % 2, h, :]
                    a.activation(t_out[:, :] if h == 0 else misc_ps[:, 0:PX], r, ACT.Identity, accum_out=sums[:, h, k:k + 1])
                    ins = a.activation(r, r, ACT.Square, accum_out=sums[:, 2 + h, k:k + 1])
                ins.then_inc(stat_done, 1)

            def sums_x1(b, i):
                s = b * STEPS + i
                act.wait_ge(x1_min, s + 1)
                if i == 0 and counts(b):
                    act.wait_ge(sums_kept, b)
                if counts(s):
                    act.wait_ge(x1_sums, s)
                a.activation(junk[:, :], xres[:, i % 2, :], ACT.Identity, accum_out=st_image[:, 0, i:i + 1])
                a.activation(junk2[:, :], xres[:, i % 2, :], ACT.Square, accum_out=st_image[:, 1, i:i + 1]).then_inc(x1_sums, 1)

            def keep_sums(b):
                act.wait_ge(x1_sums, (b + 1) * STEPS)
                one = slice(b, b + 1) if isinstance(b, int) else bass.ds(b, 1)
                a.activation(st_all[:, 0:2, one, :].rearrange("p t b n -> p t (b n)"), st_image[:, 0:2, :], ACT.Copy).then_inc(sums_kept, 1)

            def normalise_first(k):
                if k >= 4:
                    act.wait_ge(xn_first_stored[k % 4], 32)
                    act.wait_ge(t_ps, k - 3)
                for h in range(2):
                    inner = xn_first[k % 4][:, h, :].rearrange("p (r c) -> p r c", c=PW)[:, :, PAD:PAD + HW]
                    ins = a.activation(inner, x_first[:, h, k * PX:(k + 1) * PX].rearrange("p (r c) -> p r c", c=HW),
                                       ACT.Identity, bias=cf[:, 14 + h:15 + h], scale=cf[:, 12 + h:13 + h])
                ins.then_inc(norm_done, 1)

            def bias_first(k):
                act.wait_ge(t_ps, k + 1)
                if k >= 3:
                    act.wait_ge(t_first_stored[k % 3], k // 3 * 16)
                a.activation(t_first[k % 3], first_bank(k), ACT.Identity, bias=b1c).then_inc(t_ready, 1)

            def root(b):
                act.wait_ge(var_ready, b + 1)
                a.activation(cf[:, 10:12], cf[:, 8:10], ACT.Sqrt).then_inc(std_ready, 1)

            def image(b, first, last):
                for i in range(STEPS):
                    h = i // NK
                    s = b * STEPS + i
                    for kind, n in ORDER:
                        q = quad_of(kind, n)
                        bias = b2c[:, h * 13 + q:h * 13 + q + 1]
                        if kind == "D":
                            act.wait_ge(d_made, s * ND + n + 1)
                            w = wt_ps[:, n % DRING, 0:PX]
                            a.activation(w, w, ACT.Identity, bias=bias).then_inc(d_biased, 1)
                        else:
                            act.wait_ge(s_made, s * NS + n + 1)
                            if counts(s * NS + n - 1):
                                act.wait_ge(s_used, s * NS + n - 1)
                            a.activation(wt_sb[:, (i + n) % 2, :], sb_ps[:, 0:PX], ACT.Identity, bias=bias).then_inc(s_biased, 1)
                        if (kind, n) == ("S", 3) and not (first and i == 0):
                            sums_x1(*((b, i - 1) if i else (b - 1, STEPS - 1)))
                        if (kind, n) == ("D", 7) and i == 0 and not first:
                            keep_sums(b - 1)
                        if last:
                            continue
                        if (kind, n) == ("D", 2) and i == NK:
                            root(b + 1)
                        if (kind, n) == ("D", 3) and i < NK:
                            stats(b + 1, i)
                        if (kind, n) == ("D", 4) and i >= NK:
                            normalise(b + 1, i - NK)
                        if (kind, n) == ("D", 6) and i >= NK:
                            bias_t(b + 1, i - NK)

            act.wait_ge(sums_zero, 1)
            act.wait_ge(x_first_in, 32)
            for h in range(2):
                if h == 1:
                    act.wait_ge(squares_one, 1)
                ins = a.activation(square_out, x_first[:, h, :], ACT.Square, accum_out=sums[:, 2 + h, 0:1])
                ins.then_inc(squares_done if h else squares_one, 1)
            root(0)
            act.wait_ge(ones_set, 1)
            act.wait_ge(const_in, 80)
            act.wait_ge(coef_done, 1)
            normalise_first(0)
            for k in range(NK):
                if k + 1 < NK:
                    normalise_first(k + 1)
                bias_first(k)
            for r in range(5):
                n = 1024 if r < 4 else 512
                act.wait_ge(wq_ps, r + 1)
                a.activation(wqT_stage[:, r * 1024:r * 1024 + n], wt_ps[:, r % 4, :].bitcast(bf16)[:, 0:n], ACT.Copy).then_inc(wq_sb, 1)
            act.wait_ge(wq_sb, 5)
            act.dma_start(wq_d, wqT_stage).then_inc(wq_stored, 16)
            image(0, True, False)
            with act.Fori(1, B - 1) as b:
                image(b, False, False)
            image(B - 1, False, True)

            sums_x1(B - 1, STEPS - 1)
            keep_sums(B - 1)

            NI = 2 * B
            w = [raw[:, 0, 1, NI * n:NI * (n + 1)] for n in range(24)]
            small = raw[:, 1, 1, :]
            act.wait_ge(gsum_in, 2)
            a.activation(w[2], w[1], ACT.Sqrt).then_inc(gstd, 1)
            act.wait_ge(gsum_in, 4)
            a.activation(small[:, 0:B], w[13][:, B:2 * B], ACT.Sqrt).then_inc(gstd, 1)
            aa, bb, ys = raw[:, 0, 1, 8 * NI:9 * NI], raw[:, 0, 1, 9 * NI:10 * NI], small[:, 21:22]

            def affine_of(b, pairs, q, par):
                half, h = divmod(q, 2)
                act.wait_ge(x1_in[par], (pairs + 1) * 32)
                if counts(b * 4 + q - 1):
                    act.wait_ge(q_ready, b * 4 + q - 1)
                c = b * 2 + h
                one = slice(c, c + 1) if isinstance(c, int) else bass.ds(c, 1)
                src = x1b(par)[:, h, half * HALF:(half + 1) * HALF]
                a.activation(qtmp(q), src, ACT.Identity, bias=shown[:, 1, h:h + 1], scale=shown[:, 0, h:h + 1]).then_inc(act_q, 1)

            shown = raw[:, 1, 0, 64:68].rearrange("p (t h) -> p t h", t=2)

            def show(b, pairs):
                c = b * 2
                two = slice(c, c + 2) if isinstance(c, int) else bass.ds(c, 2)
                if counts(b * 4):
                    act.wait_ge(act_q, b * 4)
                a.activation(shown[:, 0, :], aa[:, two], ACT.Copy)
                a.activation(shown[:, 1, :], bb[:, two], ACT.Copy).then_inc(shown_ready, 1)
                act.wait_ge(shown_ready, b + 1)

            def outputs(b, pairs, par, more):
                for n in range(TILES):
                    k, m = divmod(n, 2)
                    tile = TILES * par + n
                    slot = tile % 4
                    act.wait_ge(conv_done, b * TILES + n + 1)
                    if counts((pairs * (2 * TILES // 4) + tile // 4) * 16):
                        act.wait_ge(y_stored[slot], (pairs * (2 * TILES // 4) + tile // 4) * 16)
                    a.activation(ybuf(slot), conv_bank(slot), ACT.Identity, bias=bias_c[:, m:m + 1], scale=ys).then_inc(y_scaled, 1)
                    if more and n in (0, 2, 4, 6):
                        if n == 0:
                            show(b + 1, pairs + par)
                        affine_of(b + 1, pairs + par, n // 2, 1 - par)

            act.wait_ge(affine_ready, 1)
            show(0, 0)
            for q in range(4):
                affine_of(0, 0, q, 0)
            for par in range(2):
                outputs(par, 0, par, True)
            with act.Fori(1, B // 2 - 1) as j:
                for par in range(2):
                    outputs(j * 2 + par, j, par, True)
            for par in range(2):
                outputs(B - 2 + par, B // 2 - 1, par, par == 0)

        @block.tensor
        def _(pe):
            mm = nc.tensor.matmul

            def group_mean(b):
                pe.wait_ge(coef_in, b + 1)
                mm(misc_ps[:, 0:4], mask[:, :], cf[:, 0:4], start=True, stop=True).then_inc(coef_ps, 1)

            def make_t(b, k):
                pe.wait_ge(norm_done, b * NK + k + 1)
                if counts(b * NK + k):
                    pe.wait_ge(t_ready, b * NK + k)
                for h in range(2):
                    inner = xn[:, h, :].rearrange("p (r c) -> p r c", c=PW)[:, :, PAD:PAD + HW]
                    ins = mm(misc_ps[:, 0:PX], w1T[:, h, :], inner, start=h == 0, stop=h == 1)
                ins.then_inc(t_ps, 1)

            def make(b, i, kind, n):
                s = b * STEPS + i
                if (kind, n) == ("D", 0):
                    pe.wait_ge(tin_in[i % 2], (b * NK + i // 2 + 1) * 16)
                lhsT = w2T[:, i // NK, quad_of(kind, n), :]
                if kind == "D":
                    if counts(s * ND + n + 1 - DRING):
                        pe.wait_ge(d_mult, s * ND + n + 1 - DRING)
                    mm(wt_ps[:, n % DRING, 0:PX], lhsT, t_in[:, i % 2, :], start=True, stop=True).then_inc(d_made, 1)
                else:
                    if counts(s * NS + n):
                        pe.wait_ge(s_biased, s * NS + n)
                    mm(sb_ps[:, 0:PX], lhsT, t_in[:, i % 2, :], start=True, stop=True).then_inc(s_made, 1)

            def add(b, i, kind, n, start, stop):
                s = b * STEPS + i
                if kind == "D":
                    if n == PAIR[1]:
                        pe.wait_ge(pair_sum, s + 1)
                    else:
                        pe.wait_ge(d_mult, s * ND + n + 1)
                    buf, done = n % DRING, d_added
                else:
                    pe.wait_ge(s_used, s * NS + n + 2)
                    buf, done = DRING + n % PRING, p_added
                if start:
                    if counts(s - 1):
                        pe.wait_ge(x1_ready, s - 1)
                for j in range(4):
                    ins = mm(acc_ps[32 * j:32 * j + 32, i % 2, 0:PX], sel[:, :], prod[:, buf, j * PX:(j + 1) * PX],
                             start=start, stop=stop)
                ins.then_inc(done, 1)

            SEQ = [("w", 0, "S", 2), ("w", 0, "D", 4), ("w", 0, "D", 5), ("a", "D", 0), ("a", "D", 1),
                   ("w", 0, "S", 3), ("w", 0, "D", 6), ("t",), ("a", "P", 0), ("a", "D", 2),
                   ("w", 0, "D", 7), ("w", 0, "S", 4), ("a", "P", 1), ("a", "D", 3),
                   ("w", 1, "D", 0), ("g",), ("w", 1, "D", 1), ("a", "D", 4), ("a", "P", 2),
                   ("w", 1, "S", 0), ("w", 1, "D", 2), ("a", "D", 7),
                   ("w", 1, "S", 1), ("w", 1, "D", 3), ("a", "P", 3), ("a", "D", 6)]

            def image(b, first, last):
                for i in range(STEPS):
                    for e in SEQ:
                        if e[0] == "g":
                            if i == NK - 1 and not last:
                                group_mean(b + 1)
                            continue
                        if e[0] == "t":
                            if i >= NK and not last:
                                make_t(b + 1, i - NK)
                        elif e[0] == "a":
                            add(b, i, e[1], e[2], e[1:] == ("D", 0), e[1:] == ("D", 6))
                        elif e[1] == 0:
                            make(b, i, e[2], e[3])
                        elif i + 1 < STEPS:
                            make(b, i + 1, e[2], e[3])
                        elif not last:
                            make(b + 1, 0, e[2], e[3])

            pe.wait_ge(const_in, 80)
            group_mean(0)
            pe.wait_ge(w2_in, 32)
            for r in range(K):
                if counts(r - 3):
                    pe.wait_ge(setup_sb, r - 3)
                for c in range(K):
                    t = r * K + c
                    ins = nc.tensor.transpose(wt_ps[:, r % 4, c * G:(c + 1) * G], w2_raw[:, t * 128:(t + 1) * 128], ident[0:G, 0:G])
                ins.then_inc(setup_ps, 1)
            pe.wait_ge(ones_set, 1)
            for h in range(2):
                for q in range(13):
                    taps = quad_taps(q)
                    for j in range(4):
                        o = h * 32 * TAPS + taps[j]
                        ins = mm(sb_ps[32 * j:32 * j + 32, h * 13 + q:h * 13 + q + 1], view(b2_row[:, o:o + 1], [[TAPS, 32]]),
                                 ones[0:1, 0:1], start=True, stop=True)
            ins.then_inc(setup_ps, 1)
            pe.wait_ge(ones_set, 3)
            for h in range(2):
                ins = nc.tensor.transpose(acc_ps[:, 0, h * 128:(h + 1) * 128], w1_ordered[:, h * 128:(h + 1) * 128], ident[:, :])
            ins.then_inc(setup_ps, 1)
            pe.wait_ge(setup_sb, 9)
            for k in range(NK):
                pe.wait_ge(norm_done, k + 1)
                if k >= 2:
                    pe.wait_ge(t_ready, k - 1)
                for h in range(2):
                    inner = xn_first[k % 4][:, h, :].rearrange("p (r c) -> p r c", c=PW)[:, :, PAD:PAD + HW]
                    ins = mm(first_bank(k), w1T[:, h, :], inner, start=h == 0, stop=h == 1)
                ins.then_inc(t_ps, 1)
            pe.wait_ge(abs_sum, 1)
            mm(sb_ps[:, 64:65], ones[:, :], cf[:, 24:25], start=True, stop=True).then_inc(abs_ps, 1)
            pe.wait_ge(wq_ready, 1)
            pe.wait_ge(ones_set, 2)
            for r in range(5):
                if counts(r - 3):
                    pe.wait_ge(wq_sb, r - 3)
                for n in range(8 if r < 4 else 4):
                    o = (r * 8 + n) * 128
                    src = wq_ordered[:, o:o + 128]
                    ins = nc.tensor.transpose(wt_ps[:, r % 4, :].bitcast(bf16)[:, n * 128:(n + 1) * 128], src, ident_b)
                ins.then_inc(wq_ps, 1)
            pe.wait_ge(wq_sb, 5)
            for kind, n in ORDER[:AHEAD]:
                make(0, 0, kind, n)
            image(0, True, False)
            with pe.Fori(1, B - 1) as b:
                image(b, False, False)
            image(B - 1, False, True)

            NI = 2 * B
            small = raw[:, 1, 1, :]
            pe.wait_ge(gsum_in, 1)
            mm(misc_ps[:, 0:2 * NI], mask[:, :], raw[:, 0, 0, 64:64 + 2 * NI], start=True, stop=True).then_inc(gsum_ps, 1)
            pe.wait_ge(gsum_in, 3)
            mm(misc_ps[:, 64:64 + 2 * B], ones[:, :], raw[:, 0, 1, 12 * NI:13 * NI], start=True, stop=True).then_inc(gsum_ps, 1)
            pe.wait_ge(gsum_in, 5)
            pe.wait_ge(ident_in, 16)
            mm(misc_ps[0:1, 128:256], small[:, 16:17], ident2, start=True, stop=True).then_inc(gsum_ps, 1)
            pe.wait_ge(gsum_in, 6)
            mm(misc_ps[:, 256:257], ones[0:1, :], small[0:1, 18:19], start=True, stop=True).then_inc(gsum_ps, 1)

            def conv(b, par):
                for n in range(TILES):
                    k, m = divmod(n, 2)
                    if n == 0:
                        pe.wait_ge(q_ready, b * 4 + 2)
                    if n == 2 * ((HW // 2 - ROWS - 1) // ROWS + 1):
                        pe.wait_ge(q_ready, b * 4 + 4)
                    slot = (TILES * par + n) % 4
                    if counts(b * TILES + n - 3):
                        pe.wait_ge(y_scaled, b * TILES + n - 3)
                    c = 0
                    for kh in range(2):
                        src = xq(par)[:, kh, :].rearrange("p (r c) -> p r c", c=CW)
                        for tap in range(KK):
                            dy, dx = divmod(tap, 3)
                            o = ((m * 2 + kh) * KK + tap) * 128
                            ins = mm(conv_bank(slot), wqT[:, o:o + 128], src[:, ROWS * k + dy:ROWS * k + dy + ROWS, dx:dx + HW],
                                     start=c == 0, stop=c == 2 * KK - 1)
                            c += 1
                    ins.then_inc(conv_done, 1)

            pe.wait_ge(wq_in, 16)
            for par in range(2):
                conv(par, par)
            with pe.Fori(1, B // 2) as j:
                for par in range(2):
                    conv(j * 2 + par, par)


_INS = ["x", "L0_conv_w1", "L0_conv_b1", "L0_conv_w2", "L0_conv_b2", "L1_conv_weight", "L1_conv_bias",
        "L1_conv_ln_weight", "L1_conv_ln_bias"]


def kernel(**inputs):
    import numpy as _np
    import concourse.bacc as _bacc
    from concourse import mybir as _mybir
    from concourse.bass_utils import run_bass_kernel_spmd as _run

    nc = _bacc.Bacc("TRN2", target_bir_lowering=False, num_devices=1)
    part = _np.arange(128)
    shapes = {
        "ident": _np.eye(128, dtype=_np.float32),
        "sel": (part[:, None] % 32 == _np.arange(32)[None, :]).astype(_np.float32),
        "mask": ((part[:, None] % 32) // 2 == (part[None, :] % 32) // 2).astype(_np.float32) / 8,
    }
    arrays, args = {}, []
    for name, a in [(n, inputs[n]) for n in _INS] + list(shapes.items()):
        a = _np.ascontiguousarray(a)
        arrays[f"in_{name}"] = a
        args.append(nc.dram_tensor(f"in_{name}", a.shape, _mybir.dt.from_np(a.dtype), kind="ExternalInput").ap())
    args.append(nc.dram_tensor("out_y", (B, C, HW, HW), _mybir.dt.float32, kind="ExternalOutput").ap())
    build(nc, *args)
    r = _run(nc, [arrays], core_ids=[0])
    return r.results[0]["out_y"]
```

```python
from contextlib import ExitStack

import numpy as np

import concourse.bass as bass
from concourse import mybir

B, C, HW = 8, 256, 56
PIX = HW * HW
RC = 128
K, PAD = 7, 3
TAPS = K * K
PW = HW + 2 * PAD
PN = PW * PW
ROWS = 8
NK = HW // ROWS
PX = ROWS * HW
PCH = ROWS * PW
STEPS = 2 * NK
VROWS = PW - 3
HLEN = PN - 3
G = C // 4
GN_EPS = 1e-5
Q_B = 128.0
MAGIC = 1.5 * 2.0 ** 23
CW = HW + 2
CN = CW * CW
KK = 9
TILES = 2 * NK

QUADS = ([("H", r, 0) for r in (0, 1, 2)] + [("V", 0, c) for c in (4, 5, 6)]
         + [("H", r, 3) for r in (4, 5, 6)] + [("V", 3, c) for c in (0, 1, 2)])
CENTRE = 12
DQ = [0, 1, 3, 4, 6, 7, 9, 10]
PQ = [2, 5, 8, 11]
ND, NP = len(DQ), len(PQ)
NS = NP + 1
DRING, PRING = 4, 2
PAIR = (5, 6)
EXTRA = (2, 3)
POOL_FROM = 2
POOL_AFTER = 2

PIECES = [(0, HW // 2), (HW // 2, HW)]
FIRST_PIECES = [(0, ROWS + 1), (ROWS + 1, HW // 2), (HW // 2, HW)]


def pieces(b):
    return FIRST_PIECES if isinstance(b, int) and b == 0 else PIECES


def pieces_before(b):
    return 0 if isinstance(b, int) and b == 0 else b * 2 * len(PIECES) + 2 * (len(FIRST_PIECES) - len(PIECES))


def extra(i, last):
    return i >= NK and not last


def adds(i, last):
    order = [0, 1, 2, 3, 4, 7, 6]
    return [n for n in order if not (extra(i, last) and n == EXTRA[0])]


def adds_before(b, i, last):
    return b * sum(len(adds(j, False)) for j in range(STEPS)) + sum(len(adds(j, last)) for j in range(i))


def extras_before(b, i, last):
    return b * NK + (0 if last else max(0, i - NK))


def pairs_before(b, i, last):
    return b * STEPS + i + extras_before(b, i, last)


def quad_taps(q):
    if q == CENTRE:
        return [PAD * K + PAD] * 4
    kind, r, c = QUADS[q]
    return [(r * K + c + s) if kind == "H" else ((r + s) * K + c) for s in range(4)]


def build(nc, x, w1, b1, w2, b2, cw, cbias, lnw, lnb, ident_d, sel_d, mask_d, out):
    f32 = mybir.dt.float32
    bf16 = mybir.dt.bfloat16
    ALU = mybir.AluOpType
    ACT = mybir.ActivationFunctionType
    AX = mybir.AxisListType.X

    xs = x.rearrange("b (h g s) r w -> b h s g (r w)", h=2, s=4)
    outs = out.rearrange("b (h g s) r w -> b h s g (r w)", h=2, s=4)
    xn_d = nc.dram_tensor("xn_padded", (B, C, PN), f32).ap()
    xns = xn_d.rearrange("b (h g s) n -> b h s g n", h=2, s=4)
    t_d = nc.dram_tensor("t_all", (B, RC, PIX), f32).ap()
    x1_d = nc.dram_tensor("x1_all", (B, 2, 128, PIX), f32).ap()
    wq_d = nc.dram_tensor("wq_all", (128, 4 * KK * 128), bf16).ap()

    nc.disable_value_cache = True
    ctx = ExitStack()
    with ctx:
        def sb(name, shape, dt=f32):
            return ctx.enter_context(nc.sbuf_tensor(name, shape, dt))

        def ps(name, shape):
            return ctx.enter_context(nc.psum_tensor(name, shape, f32))

        def sem(name):
            return ctx.enter_context(nc.semaphore(name))

        def counts(value):
            return not isinstance(value, int) or value > 0

        def view(ap, dims):
            return bass.AP(ap.tensor, ap.offset, [list(ap.ap[0])] + dims)

        shift_rows = sb("shift_rows", [128, 4, VROWS * PW])
        shift_cols = sb("shift_cols", [128, 4, HLEN])
        prod = sb("prod", [128, DRING + PRING, 4 * PX])
        w2T = sb("w2T", [128, 2, 13, 128])
        w1T = sb("w1T", [128, 2, 128])
        wt_sb = sb("wt_sb", [128, 2, PX])
        t_in = sb("t_in", [128, 2, PX])
        xres = sb("xres", [128, 2, PX])
        xc = sb("xc", [128, 2, PCH])
        raw = sb("raw", [128, 2, 2, PX])
        xn = sb("xn", [128, 2, PCH])
        t_out = sb("t_out", [128, PX])
        mask = sb("mask", [128, 128])
        ones = sb("ones", [128, 128])
        sel = sb("sel", [128, 32])
        b2c = sb("b2c", [128, 26])
        cols = sb("cols", [128, 8])
        b1c, lnw_c, lnb_c, bias_c = cols[:, 0:1], cols[:, 1:3], cols[:, 3:5], cols[:, 5:7]
        sums = sb("sums", [128, 4, NK])
        cf = sb("cf", [128, 32])
        st_image = sb("st_image", [128, 4, STEPS])
        st_all = sb("st_all", [128, 4, B, STEPS])
        zeros = view(st_all[:, 0, 0, 0:1], [[PAD * PW, 2], [1, PAD * PW]])
        junk = sb("junk", [128, PX])
        junk2 = sb("junk2", [128, PX])

        H = shift_cols[:, :, :].rearrange("p a b -> p (a b)")
        V = shift_rows[:, :, :].rearrange("p a b -> p (a b)")
        P = prod[:, :, :].rearrange("p a b -> p (a b)")
        w2_raw = H[0:G, 0:TAPS * 128]
        w1_raw = H[:, 6272:6272 + C]
        w1_ordered = H[:, 6528:6528 + C]
        ident = P[:, 9216:9344]
        ident_b = P[:, 9344:9408].bitcast(bf16)
        x_first = V[:, 3000:3000 + 2 * PIX].rearrange("p (h n) -> p h n", h=2)
        square_out = V[:, 9300:9300 + PIX]
        t_first = [H[:, 6800 + n * PX:6800 + (n + 1) * PX] for n in range(3)]
        xn_first = [H[:, 10250 + n * 2 * PCH:10250 + (n + 1) * 2 * PCH].rearrange("p (h n) -> p h n", h=2) for n in range(4)]
        b2_row = [V[0:1, 12500:12500 + TAPS * 32], H[0:1, 8680:8680 + TAPS * 32]]
        cw_raw = P[:, 0:2 * C * KK]
        wq = P[:, 4608:6912].bitcast(bf16)
        wneg = P[:, 6912:9216].bitcast(bf16)
        wq_ordered = P[:, 0:2304].bitcast(bf16)
        wqT_stage = wq

        wt_ps = ps("wt_ps", [128, DRING, 512])
        sb_ps = ps("sb_ps", [128, 512])
        acc_ps = ps("acc_ps", [128, 2, 512])
        misc_ps = ps("misc_ps", [128, 512])

        const_in = sem("const_in")
        vec_in = sem("vec_in")
        w2_in = sem("w2_in")
        b2_in = sem("b2_in")
        x_first_in = [sem(f"x_first_in{h}") for h in range(2)]
        squares_done = sem("squares_done")
        xn_first_stored = [sem(f"xn_first_stored{n}") for n in range(4)]
        t_first_stored = [sem(f"t_first_stored{n}") for n in range(3)]
        cw_in = sem("cw_in")
        zero_set = sem("zero_set")
        sums_zero = sem("sums_zero")
        squares_one = sem("squares_one")
        zero_stored = sem("zero_stored")
        ones_set = sem("ones_set")
        w1_placed = sem("w1_placed")
        w1_ps = sem("w1_ps")
        w1_sb = sem("w1_sb")
        w2_ps = sem("w2_ps")
        w2_sb = sem("w2_sb")
        b2_ps = sem("b2_ps")
        b2_sb = sem("b2_sb")
        ident_set = sem("ident_set")
        abs_sum = sem("abs_sum")
        abs_ps = sem("abs_ps")
        wq_ready = sem("wq_ready")
        wq_ps = sem("wq_ps")
        wq_sb = sem("wq_sb")
        wq_stored = sem("wq_stored")
        chain0 = sem("chain0")
        chain1 = sem("chain1")
        raw_in = [sem(f"raw_in{p}") for p in range(2)]
        stat_done = sem("stat_done")
        coef_in = sem("coef_in")
        coef_ps = sem("coef_ps")
        var_ready = sem("var_ready")
        std_ready = sem("std_ready")
        coef_done = sem("coef_done")
        norm_done = sem("norm_done")
        t_ps = sem("t_ps")
        t_ready = sem("t_ready")
        xn_stored = sem("xn_stored")
        t_stored = sem("t_stored")
        tin_in = [sem(f"tin_in{p}") for p in range(2)]
        xc_in = [sem(f"xc_in{p}") for p in range(2)]
        xres_in = [sem(f"xres_in{p}") for p in range(2)]
        shift_in = [sem(f"shift_in{k}") for k in range(NK)]
        d_made = sem("d_made")
        s_made = sem("s_made")
        d_biased = sem("d_biased")
        s_biased = sem("s_biased")
        d_mult = sem("d_mult")
        centre_mult = sem("centre_mult")
        s_used = sem("s_used")
        pair_sum = sem("pair_sum")
        pool_pair_sum = sem("pool_pair_sum")
        d_added = sem("d_added")
        p_added = sem("p_added")
        x1_ready = sem("x1_ready")
        x1_min = sem("x1_min")
        x1_sums = sem("x1_sums")
        x1_kept = sem("x1_kept")
        sums_kept = sem("sums_kept")
        x1_stored = sem("x1_stored")
        gsum_in = sem("gsum_in")
        gsum_ps = sem("gsum_ps")
        gstd = sem("gstd")
        affine_ready = sem("affine_ready")
        border_set = sem("border_set")
        wq_in = sem("wq_in")
        x1_in = [sem(f"x1_in{p}") for p in range(2)]
        ident_in = sem("ident_in")
        shown_ready = sem("shown_ready")
        act_q = sem("act_q")
        q_ready = sem("q_ready")
        conv_done = sem("conv_done")
        y_scaled = sem("y_scaled")
        y_ready = sem("y_ready")
        y_stored = [sem(f"y_stored{p}") for p in range(4)]

        def linker(eng, s, base):
            n = [0]

            def link(ins):
                n[0] += 1
                ins.then_inc(s, 1)
                eng.wait_ge(s, base + n[0])
            return link

        def shifted(q, k):
            kind, r, c = QUADS[q]
            buf, pitch = (shift_cols, HLEN) if kind == "H" else (shift_rows, VROWS * PW)
            a = buf[:, 0, (ROWS * k + r) * PW + c:(ROWS * k + r) * PW + c + 1]
            return view(a, [[pitch, 4], [PW, ROWS], [1, HW]])

        def broadcast(wt):
            return view(wt, [[0, 4], [HW, ROWS], [1, HW]])

        def product(n):
            return view(prod[:, n % DRING, 0:1], [[PX, 4], [HW, ROWS], [1, HW]])

        def pool_product(n):
            return view(prod[:, DRING + n % PRING, 0:1], [[PX, 4], [HW, ROWS], [1, HW]])

        ORDER = [("D", 0), ("D", 1), ("S", 0), ("D", 2), ("S", 1), ("D", 3), ("S", 2), ("D", 4), ("D", 5), ("S", 3),
                 ("D", 6), ("D", 7), ("S", 4)]
        AHEAD = 6

        def first_bank(k):
            return misc_ps[:, 0:PX] if k % 2 == 0 else acc_ps[:, 1, 0:PX]

        def quad_of(kind, n):
            return DQ[n] if kind == "D" else (PQ[n - 1] if n else CENTRE)

        def x1b(par):
            return V[:, par * 2 * PIX:(par + 1) * 2 * PIX].rearrange("p (h n) -> p h n", h=2)

        XQ = CN
        def xq(par):
            return H[:, par * XQ:(par + 1) * XQ].bitcast(bf16).rearrange("p (h n) -> p h n", h=2)

        HALF = PIX // 2
        def qtmp(q):
            return H[:, 2 * XQ + (q % 2) * HALF:2 * XQ + (q % 2 + 1) * HALF]

        wqT = H[:, 2 * XQ + 2 * HALF:2 * XQ + 2 * HALF + 2 * KK * 128].bitcast(bf16)

        ident2 = xc[:, 0, 0:128]

        def ybuf(slot):
            return prod[:, slot, 0:PX]

        def conv_bank(t):
            return wt_ps[:, t, 0:PX]

        block = ctx.enter_context(nc.Block())

        @block.sync
        def _(sp):
            def load_raw(b, j):
                if 2 <= j < NK + 2:
                    sp.wait_ge(stat_done, (b - 1) * NK + (j - 2) + 1)
                else:
                    sp.wait_ge(norm_done, b * NK + (j - 2 - NK if j >= 2 else j - 2) + 1)
                k = j % NK
                for h in range(2):
                    sp.dma_start(raw[:, j % 2, h, :], xs[b, h, :, :, k * PX:(k + 1) * PX]).then_inc(raw_in[j % 2], 16)

            def store_norm(b, k):
                sp.wait_ge(norm_done, b * NK + k + 1)
                o = (ROWS * k + PAD) * PW
                for h in range(2):
                    sp.dma_start(xns[b, h, :, :, o:o + PCH], xn[:, h, :]).then_inc(xn_stored, 16)
                sp.wait_ge(t_ready, b * NK + k + 1)
                sp.dma_start(t_d[b, :, k * PX:(k + 1) * PX], t_out[:, :]).then_inc(t_stored, 16)

            def zero_rows(b):
                sp.wait_ge(zero_set, 1)
                for o in (0, PN - PAD * PW):
                    sp.dma_start(xn_d[b, :, o:o + PAD * PW].rearrange("(p q) n -> p q n", q=2),
                                 zeros).then_inc(zero_stored, 16)

            def store_first(k):
                sp.wait_ge(norm_done, k + 1)
                o = (ROWS * k + PAD) * PW
                for h in range(2):
                    sp.dma_start(xns[0, h, :, :, o:o + PCH], xn_first[k % 4][:, h, :]).then_inc(xn_first_stored[k % 4], 16)
                sp.wait_ge(t_ready, k + 1)
                sp.dma_start(t_d[0, :, k * PX:(k + 1) * PX], t_first[k % 3]).then_inc(t_first_stored[k % 3], 16)

            def wait_norm_stored(b, k):
                if isinstance(b, int) and b == 0:
                    sp.wait_ge(xn_first_stored[k % 4], (k // 4 + 1) * 32)
                else:
                    sp.wait_ge(xn_stored, ((b - 1) * NK + k + 1) * 32)

            def wait_t_stored(b, k):
                if isinstance(b, int) and b == 0:
                    sp.wait_ge(t_first_stored[k % 3], (k // 3 + 1) * 16)
                else:
                    sp.wait_ge(t_stored, ((b - 1) * NK + k + 1) * 16)

            def load_shifted(b, h, k):
                wait_norm_stored(b, k)
                o = k * PCH
                nv = PCH if k < NK - 1 else VROWS * PW - o
                nh = PCH if k < NK - 1 else HLEN - o
                src = xn_d[b, h * 128:(h + 1) * 128, :]
                for s in range(4):
                    p = slice(32 * s, 32 * s + 32)
                    for dst, n, d in ((shift_rows, nv, s * PW), (shift_cols, nh, s)):
                        sp.dma_start(dst[p, :, o:o + n], src[:, o + d:o + d + n].rearrange("(g q) n -> g q n", q=4)
                                     ).then_inc(shift_in[k], 16)

            def load_step(b, i):
                h, k = divmod(i, NK)
                wait_t_stored(b, k)
                sp.dma_start(t_in[:, i % 2, :], t_d[b, :, k * PX:(k + 1) * PX]).then_inc(tin_in[i % 2], 16)
                wait_norm_stored(b, k)
                o = (ROWS * k + PAD) * PW
                sp.dma_start(xc[:, i % 2, :], xns[b, h, :, :, o:o + PCH]).then_inc(xc_in[i % 2], 16)

            def load_xres(b, i):
                h, k = divmod(i, NK)
                sp.dma_start(xres[:, i % 2, :], xs[b, h, :, :, k * PX:(k + 1) * PX]).then_inc(xres_in[i % 2], 16)

            def store_x1(b, i):
                h, k = divmod(i, NK)
                s = b * STEPS + i
                sp.wait_ge(x1_ready, s + 1)
                sp.dma_start(x1_d[b, h, :, k * PX:(k + 1) * PX], xres[:, i % 2, :]).then_inc(x1_stored, 16)

            def image(b, first, last):
                for i in range(STEPS):
                    s = b * STEPS + i
                    if not last:
                        load_raw(b + 1, i)
                    if counts(s * ND):
                        sp.wait_ge(d_mult, s * ND)
                    if counts(s * NS):
                        sp.wait_ge(s_used, s * NS)
                    if not (last and i == STEPS - 1):
                        load_step(*((b, i + 1) if i + 1 < STEPS else (b + 1, 0)))
                    if first and i + 2 < NK:
                        load_shifted(0, 0, i + 2)
                    if first and i + 1 < B:
                        zero_rows(i + 1)
                    if first and i == B:
                        sp.wait_ge(zero_stored, B * 32)
                    if i == 0 and not first:
                        load_shifted(b, 0, NK - 1)
                    elif 1 <= i <= NK:
                        load_shifted(b, 1, i - 1)
                    elif i > NK and not last:
                        load_shifted(b + 1, 0, i - NK - 1)
                    if not (first and i == 0):
                        store_x1(*((b, i - 1) if i else (b - 1, STEPS - 1)))
                    if not (last and i == STEPS - 1):
                        if counts(s):
                            sp.wait_ge(x1_sums, s)
                        if counts(s * 16):
                            sp.wait_ge(x1_stored, s * 16)
                        load_xres(*((b, i + 1) if i + 1 < STEPS else (b + 1, 0)))
                    if i >= NK and not last:
                        store_norm(b + 1, i - NK)

            sp.dma_start(x_first[:, 0, :], xs[0, 0, :, :, :]).then_inc(x_first_in[0], 16)
            for dst, src in ((sel[:, :], sel_d), (mask[:, :], mask_d), (ident, ident_d), (w1_raw, w1),
                             (b1c, b1.rearrange("(p o) -> p o", o=1))):
                sp.dma_start(dst, src).then_inc(const_in, 16)
            sp.dma_start(x_first[:, 1, :], xs[0, 1, :, :, :]).then_inc(x_first_in[1], 16)
            sp.dma_start(w2_raw.rearrange("g (p r) -> g p r", r=128), w2.rearrange("(g p) r -> g p r", p=TAPS)).then_inc(w2_in, 16)
            for h in range(2):
                sp.dma_start(b2_row[h], b2[h * 32 * TAPS:(h + 1) * 32 * TAPS].rearrange("(a n) -> a n", a=1)).then_inc(b2_in, 16)
            for dst, src in ((lnw_c, lnw), (lnb_c, lnb), (bias_c, cbias)):
                v = src.rearrange("(h g s o) -> h s g o", h=2, s=4, o=1)
                for h in range(2):
                    sp.dma_start(dst[:, h:h + 1], v[h], allow_slow_non_contiguous=True).then_inc(vec_in, 16)
            zero_rows(0)
            cws = cw.rearrange("(m g s) i a b -> m s g (i a b)", m=2, s=4)
            for m in range(2):
                sp.dma_start(cw_raw[:, m * C * KK:(m + 1) * C * KK], cws[m]).then_inc(cw_in, 16)
            for k in range(NK):
                store_first(k)
            for n in range(4):
                sp.wait_ge(xn_first_stored[n], len(range(n, NK, 4)) * 32)
            for n in range(3):
                sp.wait_ge(t_first_stored[n], len(range(n, NK, 3)) * 16)
            sp.wait_ge(zero_stored, 32)
            sp.wait_ge(w2_ps, K)
            load_step(0, 0)
            for k in range(2):
                load_shifted(0, 0, k)
            load_xres(0, 0)
            sp.wait_ge(wq_sb, 5)
            sp.dma_start(wq_d, wqT_stage).then_inc(wq_stored, 16)
            sp.wait_ge(b2_ps, 1)
            image(0, True, False)
            with sp.Fori(1, B - 1) as b:
                image(b, False, False)
            image(B - 1, False, True)
            store_x1(B - 1, STEPS - 1)

            def load_x1(b, par):
                for h in range(2):
                    sp.dma_start(x1b(par)[:, h, :], x1_d[b, h, :, :]).then_inc(x1_in[par], 16)

            sp.wait_ge(d_mult, B * STEPS * ND)
            sp.wait_ge(s_used, B * STEPS * NS)
            sp.wait_ge(x1_stored, B * STEPS * 16)
            sp.wait_ge(wq_stored, 16)
            sp.dma_start(ident2, ident_d).then_inc(ident_in, 16)
            load_x1(0, 0)
            sp.dma_start(wqT, wq_d).then_inc(wq_in, 16)
            load_x1(1, 1)

            def stores(b, par, more):
                for n in range(TILES):
                    k, m = divmod(n, 2)
                    slot = (TILES * par + n) % 4
                    sp.wait_ge(y_ready, b * TILES + n + 1)
                    sp.dma_start(outs[b, m, :, :, k * PX:(k + 1) * PX], ybuf(slot)).then_inc(y_stored[slot], 16)
                if more:
                    load_x1(b + 2, par)

            for par in range(2):
                stores(par, par, True)
            with sp.Fori(1, B // 2 - 1) as j:
                for par in range(2):
                    stores(j * 2 + par, par, True)
            for par in range(2):
                stores(B - 2 + par, par, False)
            for slot in range(4):
                sp.wait_ge(y_stored[slot], B * TILES // 4 * 16)

        @block.vector
        def _(dve):
            v = nc.vector
            NL0 = 9

            def coef_a(b):
                dve.wait_ge(stat_done, b * NK)
                v.tensor_reduce(cf[:, 0:4], sums[:, :, :], AX, ALU.add).then_inc(coef_in, 1)

            def coef_b(b):
                link = linker(dve, chain0, b * NL0)
                dve.wait_ge(coef_ps, b + 1)
                link(v.tensor_scalar_mul(cf[:, 4:8], misc_ps[:, 0:4], 1.0 / PIX))
                link(v.tensor_tensor(cf[:, 16:18], cf[:, 4:6], cf[:, 4:6], ALU.mult))
                link(v.tensor_tensor(cf[:, 18:20], cf[:, 6:8], cf[:, 16:18], ALU.subtract))
                v.tensor_scalar_add(cf[:, 8:10], cf[:, 18:20], GN_EPS).then_inc(var_ready, 1)

            def newton(link, var, root, inv, tmp, last):
                link(v.reciprocal(inv, root))
                link(v.tensor_tensor(tmp, inv, inv, ALU.mult))
                link(v.scalar_tensor_tensor(tmp, tmp, -0.5, var, ALU.mult, ALU.mult))
                last(v.scalar_tensor_tensor(inv, tmp, 1.5, inv, ALU.add, ALU.mult))

            def coef_c(b):
                link = linker(dve, chain0, b * NL0 + 3)
                dve.wait_ge(std_ready, b + 1)
                if counts(b * NK):
                    dve.wait_ge(norm_done, b * NK)
                newton(link, cf[:, 8:10], cf[:, 10:12], cf[:, 12:14], cf[:, 16:18], link)
                link(v.tensor_tensor(cf[:, 18:20], cf[:, 4:6], cf[:, 12:14], ALU.mult))
                link(v.tensor_scalar_mul(cf[:, 14:16], cf[:, 18:20], -1.0))
                v.nop().then_inc(coef_done, 1)

            def finish(b, i, last):
                s = b * STEPS + i
                if i == 0 and counts(b):
                    dve.wait_ge(x1_kept, b)
                dve.wait_ge(d_added, adds_before(b, i + 1, last))
                dve.wait_ge(p_added, (s + 1) * NP)
                dve.wait_ge(s_used, s * NS + 1)
                v.memset(cf[:, 30:31], 0.0)
                v.tensor_tensor_reduce(out=xres[:, i % 2, :], in0=acc_ps[:, i % 2, 0:PX], in1=xres[:, i % 2, :], scale=1.0,
                                       scalar=-3.0e38, op0=ALU.add, op1=ALU.max, accum_out=st_image[:, 2, i:i + 1]).then_inc(x1_ready, 1)
                dve.wait_ge(x1_ready, s + 1)
                v.tensor_reduce(st_image[:, 3, i:i + 1], xres[:, i % 2, :], AX, ALU.min).then_inc(x1_min, 1)

            def add_pair(s, pair):
                dve.wait_ge(d_mult, s * ND + pair[1] + 1)
                end = POOL_FROM * PX if pair == EXTRA else 4 * PX
                two = [prod[:, n % DRING, 0:end] for n in pair]
                v.tensor_tensor(two[1], two[0], two[1], ALU.add).then_inc(pair_sum, 1)

            def keep_stats(b):
                dve.wait_ge(x1_min, (b + 1) * STEPS)
                one = slice(b, b + 1) if isinstance(b, int) else bass.ds(b, 1)
                v.tensor_copy(st_all[:, 2:4, one, :].rearrange("p t b n -> p t (b n)"), st_image[:, 2:4, :]).then_inc(x1_kept, 1)

            def image(b, first, last):
                for i in range(STEPS):
                    k = i % NK
                    s = b * STEPS + i
                    phase = b * 2 + i // NK
                    for n in range(ND):
                        if first and i == 0 and n == 2:
                            dve.wait_ge(wq_stored, 16)
                        if n == 0:
                            for kk in (k, k + 1)[:2 if k + 1 < NK else 1]:
                                dve.wait_ge(shift_in[kk], (phase + 1) * 128)
                        dve.wait_ge(d_biased, s * ND + n + 1)
                        if n < DRING and n % DRING != PAIR[0] % DRING:
                            if not (first and i == 0):
                                pb, pi = (b, i - 1) if i else (b - 1, STEPS - 1)
                                plast = last and i > 0
                                dve.wait_ge(d_added, adds_before(pb, pi, plast) + adds(pi, plast).index(n + DRING) + 1)
                        elif n < DRING:
                            if not (first and i == 0):
                                dve.wait_ge(pair_sum, pairs_before(b, i, last))
                        elif extra(i, last) and n - DRING == EXTRA[0]:
                            dve.wait_ge(pair_sum, pairs_before(b, i, last) + 1)
                            dve.wait_ge(pool_pair_sum, extras_before(b, i, last) + 1)
                        else:
                            dve.wait_ge(d_added, adds_before(b, i, last) + adds(i, last).index(n - DRING) + 1)
                        v.tensor_tensor(product(n), broadcast(wt_ps[:, n % DRING, 0:PX]), shifted(DQ[n], k), ALU.mult
                                        ).then_inc(d_mult, 1)
                        if n == 1 and i == NK and not last:
                            coef_c(b + 1)
                        if n == 1 and not (first and i == 0):
                            finish(*((b, i - 1, last) if i else (b - 1, STEPS - 1, False)))
                        if n == 2 and i == 0 and not first:
                            keep_stats(b - 1)
                        if n == EXTRA[1] and extra(i, last):
                            add_pair(s, EXTRA)
                        if n == 4 and i == NK - 1 and not last:
                            coef_a(b + 1)
                    add_pair(s, PAIR)
                    if i == NK - 1 and not last:
                        coef_b(b + 1)

            v.memset(sums[:, :, :], 0.0).then_inc(sums_zero, 1)
            dve.wait_ge(const_in, 80)
            for h in range(2):
                last_copy = v.tensor_copy(view(w1_ordered[:, h * 128:h * 128 + 1], [[32, 4], [1, 32]]),
                                          view(w1_raw[:, h * 128:h * 128 + 1], [[1, 4], [4, 32]]))
            last_copy.then_inc(w1_placed, 1)
            v.tensor_copy(ident_b, ident).then_inc(ident_set, 1)
            dve.wait_ge(w1_ps, 1)
            v.tensor_copy(w1T[:, :, :].rearrange("p a b -> p (a b)"), acc_ps[:, 0, 0:256]).then_inc(w1_sb, 1)
            dve.wait_ge(sums_zero, 1)
            for h in range(2):
                dve.wait_ge(x_first_in[h], 16)
                ins = v.tensor_reduce(sums[:, h, 0:1], x_first[:, h, :], AX, ALU.add)
            ins.then_inc(squares_done, 1)
            dve.wait_ge(squares_done, 2)
            v.tensor_reduce(cf[:, 0:4], sums[:, :, :], AX, ALU.add).then_inc(coef_in, 1)
            coef_b(0)
            coef_c(0)
            where = {t: [(q, s) for q in range(13) for s, u in enumerate(quad_taps(q)) if u == t] for t in range(TAPS)}
            for r in range(K):
                dve.wait_ge(w2_ps, r + 1)
                for c in range(K):
                    src = wt_ps[:, r % 4, c * G:(c + 1) * G].rearrange("p (h g) -> p h g", h=2)
                    for q, s in where[r * K + c]:
                        last_copy = v.tensor_copy(w2T[:, :, q, 32 * s:32 * s + 32], src)
                last_copy.then_inc(w2_sb, 1)
            dve.wait_ge(cw_in, 32)
            v.tensor_reduce(cf[:, 24:25], cw_raw, AX, ALU.add, apply_absolute_value=True).then_inc(abs_sum, 1)
            dve.wait_ge(abs_ps, 1)
            wl = linker(dve, chain1, 0)
            wl(v.tensor_scalar(cf[:, 25:26], acc_ps[:, 0, 256:257], 1.0 / (C * C * KK), 0.7, ALU.mult, ALU.mult))
            wl(v.tensor_scalar_mul(cf[:, 26:27], cf[:, 25:26], -1.0))
            wl(v.tensor_scalar(wq, cw_raw, cf[:, 25:26], None, ALU.is_gt))
            wl(v.tensor_scalar(wneg, cw_raw, cf[:, 26:27], None, ALU.is_lt))
            for mk in range(4):
                o = mk * KK * 128
                src = [view(a[:, o:o + 1], [[KK, 4], [4 * KK, 32], [1, KK]]) for a in (wq, wneg)]
                ins = v.tensor_tensor(view(wq_ordered[:, o:o + 1], [[32, 4], [1, 32], [128, KK]]), src[0], src[1], ALU.subtract)
            ins.then_inc(wq_ready, 1)
            dve.wait_ge(b2_ps, 1)
            v.tensor_copy(b2c[:, :], sb_ps[:, 0:26]).then_inc(b2_sb, 1)
            dve.wait_ge(wq_ps, 5)

            image(0, True, False)
            dve.wait_ge(zero_stored, B * 32)
            with dve.Fori(1, B - 1) as b:
                image(b, False, False)
            image(B - 1, False, True)
            finish(B - 1, STEPS - 1, True)
            keep_stats(B - 1)

            dve.wait_ge(vec_in, 96)
            link = linker(dve, chain1, 4)
            NI = 2 * B
            g2 = raw[:, 0, 0, 64:64 + 2 * NI]
            w = [raw[:, 0, 1, NI * n:NI * (n + 1)] for n in range(24)]
            gm, gv, root, rg, tmp, dd, e1, e2, aa, bb, mxr, mnr = w[:12]
            var_c = w[15]
            uu = w[13]
            rgw, shift = w[16], w[17]
            extremes = view(mxr, [[NI, 2], [1, NI]])
            small = raw[:, 1, 1, :]
            by_half = st_all[:, :, :, :].rearrange("p t b (h k) -> p t (b h) k", h=2)
            dve.wait_ge(x1_kept, B)
            link(v.tensor_reduce(mxr, by_half[:, 2], AX, ALU.max))
            link(v.tensor_reduce(mnr, by_half[:, 3], AX, ALU.min))
            dve.wait_ge(sums_kept, B)
            link(v.tensor_reduce(g2, by_half[:, 0:2].rearrange("p t n k -> p (t n) k"), AX, ALU.add))
            link(v.tensor_scalar_mul(g2, g2, 1.0 / PIX))
            v.nop().then_inc(gsum_in, 1)
            m1, m2 = g2[:, 0:NI], g2[:, NI:2 * NI]
            link(v.tensor_tensor(e2, m1, m1, ALU.mult))
            link(v.tensor_tensor(var_c, m2, e2, ALU.subtract))
            dve.wait_ge(gsum_ps, 1)
            link(v.tensor_copy(gm, misc_ps[:, 0:NI]))
            link(v.tensor_tensor(tmp, gm, gm, ALU.mult))
            link(v.scalar_tensor_tensor(gv, misc_ps[:, NI:2 * NI], GN_EPS, tmp, ALU.add, ALU.subtract))
            v.nop().then_inc(gsum_in, 1)
            link(v.tensor_tensor(dd, m1, gm, ALU.subtract))
            link(v.tensor_tensor(e2, dd, dd, ALU.mult))
            link(v.tensor_tensor(var_c, e2, var_c, ALU.add))
            dve.wait_ge(gstd, 1)
            newton(link, gv, root, rg, tmp, link)
            v.tensor_tensor(e1, dd, rg, ALU.mult)
            link(v.tensor_tensor(tmp, rg, rg, ALU.mult))
            link(v.tensor_tensor(e2, var_c, tmp, ALU.mult))
            v.nop().then_inc(gsum_in, 1)

            def per_image(a):
                return view(a, [[1, B], [0, 2]])

            def per_half(a):
                return view(a, [[0, B], [1, 2]])

            def three(a):
                return view(a, [[2, B], [1, 2]])

            v.tensor_tensor(three(rgw), three(rg), per_half(lnw_c), ALU.mult)
            link(v.tensor_tensor(shift, gm, rg, ALU.mult))
            dve.wait_ge(gsum_ps, 2)
            link(v.tensor_scalar_mul(uu, misc_ps[:, 64:64 + 2 * B], 1.0 / C))
            mu, v2 = uu[:, 0:B], uu[:, B:2 * B]
            link(v.tensor_tensor(tmp[:, 0:B], mu, mu, ALU.mult))
            link(v.scalar_tensor_tensor(v2, v2, GN_EPS, tmp[:, 0:B], ALU.add, ALU.subtract))
            v.nop().then_inc(gsum_in, 1)
            link(v.tensor_tensor(three(shift), three(shift), per_image(mu), ALU.add))
            link(v.tensor_tensor(three(shift), three(shift), per_half(lnw_c), ALU.mult))
            dve.wait_ge(gstd, 2)
            r2 = w[14][:, 0:B]
            newton(link, v2, small[:, 0:B], r2, tmp[:, 0:B], link)
            v.tensor_tensor(three(aa), three(rgw), per_image(r2), ALU.mult)
            link(v.tensor_tensor(three(tmp), three(shift), per_image(r2), ALU.mult))
            link(v.tensor_tensor(three(bb), per_half(lnb_c), three(tmp), ALU.subtract))
            both = [view(c, [[0, 2], [1, NI]]) for c in (aa, bb)]
            link(v.tensor_tensor(extremes, extremes, both[0], ALU.mult))
            link(v.tensor_tensor(extremes, extremes, both[1], ALU.add))
            link(v.tensor_reduce(small[:, 16:17], raw[:, 0, 1, 10 * NI:12 * NI], AX, ALU.max, apply_absolute_value=True))
            v.nop().then_inc(gsum_in, 1)
            dve.wait_ge(gsum_ps, 3)
            link(v.tensor_reduce(small[0:1, 17:18], misc_ps[0:1, 128:256], AX, ALU.max))
            link(v.tensor_scalar_max(small[0:1, 18:19], small[0:1, 17:18], 1e-6))
            v.nop().then_inc(gsum_in, 1)
            dve.wait_ge(gsum_ps, 4)
            rq, ys = small[:, 20:21], small[:, 21:22]
            v.tensor_scalar(ys, misc_ps[:, 256:257], 1.0 / Q_B, 0.01, ALU.mult, ALU.mult)
            link(v.reciprocal(rq, misc_ps[:, 256:257]))
            v.tensor_scalar(aa, aa, rq, Q_B, ALU.mult, ALU.mult)
            link(v.tensor_scalar(bb, bb, rq, Q_B, ALU.mult, ALU.mult))
            v.nop().then_inc(affine_ready, 1)

            def quantise(b, q, par):
                piece, h = divmod(q, 2)
                lo, hi = pieces(b)[piece]
                scaled = qtmp(q)[:, 0:(hi - lo) * HW]
                lq = linker(dve, chain0, B * NL0 + (pieces_before(b) + q) * 2)
                dve.wait_ge(act_q, pieces_before(b) + q + 1)
                if q == 0:
                    if counts((b - 1) * TILES):
                        dve.wait_ge(conv_done, (b - 1) * TILES)
                lq(v.tensor_scalar(scaled, scaled, MAGIC, MAGIC, ALU.add, ALU.subtract))
                inner = xq(par)[:, h, :].rearrange("p (r c) -> p r c", c=CW)[:, 1 + lo:1 + hi, 1:1 + HW]
                lq(v.tensor_scalar(inner, scaled.rearrange("p (r c) -> p r c", c=HW), Q_B, -Q_B, ALU.min, ALU.max))
                v.nop().then_inc(q_ready, 1)

            def outputs(b, par, more):
                for n in range(TILES):
                    k, m = divmod(n, 2)
                    slot = (TILES * par + n) % 4
                    dve.wait_ge(y_scaled, b * TILES + n + 1)
                    v.tensor_tensor(ybuf(slot), ybuf(slot), x1b(par)[:, m, k * PX:(k + 1) * PX], ALU.add).then_inc(y_ready, 1)
                    if more and n in (1, 3, 5, 7):
                        quantise(b + 1, n // 2, 1 - par)

            dve.wait_ge(border_set, 1)
            for q in range(2 * len(FIRST_PIECES)):
                quantise(0, q, 0)
            for par in range(2):
                outputs(par, par, True)
            with dve.Fori(1, B // 2 - 1) as j:
                for par in range(2):
                    outputs(j * 2 + par, par, True)
            for par in range(2):
                outputs(B - 2 + par, par, par == 0)

        @block.gpsimd
        def _(pool):
            g = nc.gpsimd

            def image(b, first, last):
                for i in range(STEPS):
                    k = i % NK
                    s = b * STEPS + i
                    phase = b * 2 + i // NK
                    par = i % 2
                    wt = wt_sb[:, i % 2, :]
                    pool.wait_ge(s_biased, s * NS + 1)
                    pool.wait_ge(xc_in[par], (b * NK + i // 2 + 1) * 16)
                    rows = lambda a: a.rearrange("p (r c) -> p r c", c=HW)
                    centre = xc[:, par, :].rearrange("p (r c) -> p r c", c=PW)[:, :, PAD:PAD + HW]
                    g.tensor_tensor(rows(wt), rows(wt), centre, ALU.mult).then_inc(centre_mult, 1)
                    pool.wait_ge(centre_mult, s + 1)
                    pool.wait_ge(xres_in[par], (b * NK + i // 2 + 1) * 16)
                    g.tensor_tensor(xres[:, par, :], xres[:, par, :], wt, ALU.add).then_inc(s_used, 1)
                    for kk in (k, k + 1)[:2 if k + 1 < NK else 1]:
                        pool.wait_ge(shift_in[kk], (phase + 1) * 128)
                    for n in range(NP):
                        if n == POOL_AFTER and extra(i, last):
                            pool.wait_ge(d_mult, s * ND + EXTRA[1] + 1)
                            two = [prod[:, m % DRING, POOL_FROM * PX:] for m in EXTRA]
                            g.tensor_tensor(two[1], two[0], two[1], ALU.add).then_inc(pool_pair_sum, 1)
                        pool.wait_ge(s_biased, s * NS + n + 2)
                        if counts(s * NP + n + 1 - PRING):
                            pool.wait_ge(p_added, s * NP + n + 1 - PRING)
                        g.tensor_tensor(pool_product(n), broadcast(wt_sb[:, (i + n + 1) % 2, :]), shifted(PQ[n], k), ALU.mult
                                        ).then_inc(s_used, 1)

            g.memset(zeros, 0.0).then_inc(zero_set, 1)
            for n in range(4):
                g.memset(xn_first[n], 0.0)
            g.memset(ones[:, :], 1.0)
            g.memset(xn[:, :, :], 0.0).then_inc(ones_set, 1)
            pool.wait_ge(wq_ps, 5)
            image(0, True, False)
            with pool.Fori(1, B - 1) as b:
                image(b, False, False)
            image(B - 1, False, True)
            pool.wait_ge(d_mult, B * STEPS * ND)
            pool.wait_ge(s_used, B * STEPS * NS)
            for par in range(2):
                ins = g.memset(H[:, par * XQ:(par + 1) * XQ], 0.0)
            ins.then_inc(border_set, 1)

        @block.scalar
        def _(act):
            a = nc.scalar

            def normalise(b, k):
                j = NK + k
                act.wait_ge(coef_done, b + 1)
                act.wait_ge(raw_in[j % 2], ((b - 1) * NK + j // 2 + 1) * 32)
                if counts((b - 1) * NK + k):
                    act.wait_ge(xn_stored, ((b - 1) * NK + k) * 32)
                act.wait_ge(t_ps, b * NK + k)
                for h in range(2):
                    inner = xn[:, h, :].rearrange("p (r c) -> p r c", c=PW)[:, :, PAD:PAD + HW]
                    ins = a.activation(inner, raw[:, j % 2, h, :].rearrange("p (r c) -> p r c", c=HW), ACT.Identity,
                                       bias=cf[:, 14 + h:15 + h], scale=cf[:, 12 + h:13 + h])
                ins.then_inc(norm_done, 1)

            def bias_t(b, k):
                act.wait_ge(t_ps, b * NK + k + 1)
                if counts((b - 1) * NK + k):
                    act.wait_ge(t_stored, ((b - 1) * NK + k) * 16)
                a.activation(t_out[:, :], misc_ps[:, 0:PX], ACT.Identity, bias=b1c).then_inc(t_ready, 1)

            def stats(b, k):
                act.wait_ge(raw_in[k % 2], ((b - 1) * NK + k // 2 + 1) * 32)
                if k == 0:
                    if counts((b - 1) * NK):
                        act.wait_ge(t_stored, (b - 1) * NK * 16)
                if counts((b - 1) * NK + k):
                    act.wait_ge(stat_done, (b - 1) * NK + k)
                for h in range(2):
                    r = raw[:, k % 2, h, :]
                    a.activation(t_out[:, :] if h == 0 else misc_ps[:, 0:PX], r, ACT.Identity, accum_out=sums[:, h, k:k + 1])
                    ins = a.activation(r, r, ACT.Square, accum_out=sums[:, 2 + h, k:k + 1])
                ins.then_inc(stat_done, 1)

            def sums_x1(b, i):
                s = b * STEPS + i
                act.wait_ge(x1_min, s + 1)
                if i == 0 and counts(b):
                    act.wait_ge(sums_kept, b)
                if counts(s):
                    act.wait_ge(x1_sums, s)
                a.activation(junk[:, :], xres[:, i % 2, :], ACT.Identity, accum_out=st_image[:, 0, i:i + 1])
                a.activation(junk2[:, :], xres[:, i % 2, :], ACT.Square, accum_out=st_image[:, 1, i:i + 1]).then_inc(x1_sums, 1)

            def keep_sums(b):
                act.wait_ge(x1_sums, (b + 1) * STEPS)
                one = slice(b, b + 1) if isinstance(b, int) else bass.ds(b, 1)
                a.activation(st_all[:, 0:2, one, :].rearrange("p t b n -> p t (b n)"), st_image[:, 0:2, :], ACT.Copy).then_inc(sums_kept, 1)

            def normalise_first(k):
                if k >= 4:
                    act.wait_ge(xn_first_stored[k % 4], 32)
                    act.wait_ge(t_ps, k - 3)
                for h in range(2):
                    inner = xn_first[k % 4][:, h, :].rearrange("p (r c) -> p r c", c=PW)[:, :, PAD:PAD + HW]
                    ins = a.activation(inner, x_first[:, h, k * PX:(k + 1) * PX].rearrange("p (r c) -> p r c", c=HW),
                                       ACT.Identity, bias=cf[:, 14 + h:15 + h], scale=cf[:, 12 + h:13 + h])
                ins.then_inc(norm_done, 1)

            def bias_first(k):
                act.wait_ge(t_ps, k + 1)
                if k >= 3:
                    act.wait_ge(t_first_stored[k % 3], k // 3 * 16)
                a.activation(t_first[k % 3], first_bank(k), ACT.Identity, bias=b1c).then_inc(t_ready, 1)

            def root(b):
                act.wait_ge(var_ready, b + 1)
                a.activation(cf[:, 10:12], cf[:, 8:10], ACT.Sqrt).then_inc(std_ready, 1)

            def image(b, first, last):
                for i in range(STEPS):
                    h = i // NK
                    s = b * STEPS + i
                    for kind, n in ORDER:
                        q = quad_of(kind, n)
                        bias = b2c[:, h * 13 + q:h * 13 + q + 1]
                        if kind == "D":
                            act.wait_ge(d_made, s * ND + n + 1)
                            w = wt_ps[:, n % DRING, 0:PX]
                            a.activation(w, w, ACT.Identity, bias=bias).then_inc(d_biased, 1)
                        else:
                            act.wait_ge(s_made, s * NS + n + 1)
                            if counts(s * NS + n - 1):
                                act.wait_ge(s_used, s * NS + n - 1)
                            a.activation(wt_sb[:, (i + n) % 2, :], sb_ps[:, 0:PX], ACT.Identity, bias=bias).then_inc(s_biased, 1)
                        if (kind, n) == ("S", 3) and not (first and i == 0):
                            sums_x1(*((b, i - 1) if i else (b - 1, STEPS - 1)))
                        if (kind, n) == ("D", 7) and i == 0 and not first:
                            keep_sums(b - 1)
                        if last:
                            continue
                        if (kind, n) == ("D", 2) and i == NK:
                            root(b + 1)
                        if (kind, n) == ("D", 3) and i < NK:
                            stats(b + 1, i)
                        if (kind, n) == ("D", 4) and i >= NK:
                            normalise(b + 1, i - NK)
                        if (kind, n) == ("D", 6) and i >= NK:
                            bias_t(b + 1, i - NK)

            act.wait_ge(sums_zero, 1)
            for h in range(2):
                act.wait_ge(x_first_in[h], 16)
                if h == 1:
                    act.wait_ge(squares_one, 1)
                ins = a.activation(square_out, x_first[:, h, :], ACT.Square, accum_out=sums[:, 2 + h, 0:1])
                ins.then_inc(squares_done if h else squares_one, 1)
            root(0)
            act.wait_ge(ones_set, 1)
            act.wait_ge(const_in, 80)
            act.wait_ge(coef_done, 1)
            normalise_first(0)
            for k in range(NK):
                if k + 1 < NK:
                    normalise_first(k + 1)
                bias_first(k)
            for r in range(5):
                n = 1024 if r < 4 else 512
                act.wait_ge(wq_ps, r + 1)
                a.activation(wqT_stage[:, r * 1024:r * 1024 + n], wt_ps[:, r % 4, :].bitcast(bf16)[:, 0:n], ACT.Copy).then_inc(wq_sb, 1)
            image(0, True, False)
            act.wait_ge(zero_stored, B * 32)
            with act.Fori(1, B - 1) as b:
                image(b, False, False)
            image(B - 1, False, True)

            sums_x1(B - 1, STEPS - 1)
            keep_sums(B - 1)

            NI = 2 * B
            w = [raw[:, 0, 1, NI * n:NI * (n + 1)] for n in range(24)]
            small = raw[:, 1, 1, :]
            act.wait_ge(gsum_in, 2)
            a.activation(w[2], w[1], ACT.Sqrt).then_inc(gstd, 1)
            act.wait_ge(gsum_in, 4)
            a.activation(small[:, 0:B], w[13][:, B:2 * B], ACT.Sqrt).then_inc(gstd, 1)
            aa, bb, ys = raw[:, 0, 1, 8 * NI:9 * NI], raw[:, 0, 1, 9 * NI:10 * NI], small[:, 21:22]

            def affine_of(b, pairs, q, par):
                piece, h = divmod(q, 2)
                lo, hi = pieces(b)[piece]
                act.wait_ge(x1_in[par], (pairs + 1) * 32)
                if counts(pieces_before(b) + q - 1):
                    act.wait_ge(q_ready, pieces_before(b) + q - 1)
                src = x1b(par)[:, h, lo * HW:hi * HW]
                a.activation(qtmp(q)[:, 0:(hi - lo) * HW], src, ACT.Identity, bias=shown[:, 1, h:h + 1], scale=shown[:, 0, h:h + 1]).then_inc(act_q, 1)

            shown = raw[:, 1, 0, 64:68].rearrange("p (t h) -> p t h", t=2)

            def show(b, pairs):
                c = b * 2
                two = slice(c, c + 2) if isinstance(c, int) else bass.ds(c, 2)
                if counts(pieces_before(b)):
                    act.wait_ge(act_q, pieces_before(b))
                a.activation(shown[:, 0, :], aa[:, two], ACT.Copy)
                a.activation(shown[:, 1, :], bb[:, two], ACT.Copy).then_inc(shown_ready, 1)
                act.wait_ge(shown_ready, b + 1)

            def outputs(b, pairs, par, more):
                for n in range(TILES):
                    k, m = divmod(n, 2)
                    tile = TILES * par + n
                    slot = tile % 4
                    act.wait_ge(conv_done, b * TILES + n + 1)
                    if counts((pairs * (2 * TILES // 4) + tile // 4) * 16):
                        act.wait_ge(y_stored[slot], (pairs * (2 * TILES // 4) + tile // 4) * 16)
                    a.activation(ybuf(slot), conv_bank(slot), ACT.Identity, bias=bias_c[:, m:m + 1], scale=ys).then_inc(y_scaled, 1)
                    if more and n in (0, 2, 4, 6):
                        if n == 0:
                            show(b + 1, pairs + par)
                        affine_of(b + 1, pairs + par, n // 2, 1 - par)

            act.wait_ge(affine_ready, 1)
            show(0, 0)
            for q in range(2 * len(FIRST_PIECES)):
                affine_of(0, 0, q, 0)
            for par in range(2):
                outputs(par, 0, par, True)
            with act.Fori(1, B // 2 - 1) as j:
                for par in range(2):
                    outputs(j * 2 + par, j, par, True)
            for par in range(2):
                outputs(B - 2 + par, B // 2 - 1, par, par == 0)

        @block.tensor
        def _(pe):
            mm = nc.tensor.matmul

            def group_mean(b):
                pe.wait_ge(coef_in, b + 1)
                mm(misc_ps[:, 0:4], mask[:, :], cf[:, 0:4], start=True, stop=True).then_inc(coef_ps, 1)

            def make_t(b, k):
                pe.wait_ge(norm_done, b * NK + k + 1)
                if counts(b * NK + k):
                    pe.wait_ge(t_ready, b * NK + k)
                for h in range(2):
                    inner = xn[:, h, :].rearrange("p (r c) -> p r c", c=PW)[:, :, PAD:PAD + HW]
                    ins = mm(misc_ps[:, 0:PX], w1T[:, h, :], inner, start=h == 0, stop=h == 1)
                ins.then_inc(t_ps, 1)

            def make(b, i, kind, n):
                s = b * STEPS + i
                if (kind, n) == ("D", 0):
                    pe.wait_ge(tin_in[i % 2], (b * NK + i // 2 + 1) * 16)
                lhsT = w2T[:, i // NK, quad_of(kind, n), :]
                if kind == "D":
                    if counts(s * ND + n + 1 - DRING):
                        pe.wait_ge(d_mult, s * ND + n + 1 - DRING)
                    mm(wt_ps[:, n % DRING, 0:PX], lhsT, t_in[:, i % 2, :], start=True, stop=True).then_inc(d_made, 1)
                else:
                    if counts(s * NS + n):
                        pe.wait_ge(s_biased, s * NS + n)
                    mm(sb_ps[:, 0:PX], lhsT, t_in[:, i % 2, :], start=True, stop=True).then_inc(s_made, 1)

            def add(b, i, kind, n, start, stop, last):
                s = b * STEPS + i
                if kind == "D":
                    if n == PAIR[1]:
                        pe.wait_ge(pair_sum, pairs_before(b, i + 1, last))
                    elif extra(i, last) and n == EXTRA[1]:
                        pe.wait_ge(pair_sum, pairs_before(b, i, last) + 1)
                        pe.wait_ge(pool_pair_sum, extras_before(b, i, last) + 1)
                    else:
                        pe.wait_ge(d_mult, s * ND + n + 1)
                    buf, done = n % DRING, d_added
                else:
                    pe.wait_ge(s_used, s * NS + n + 2)
                    buf, done = DRING + n % PRING, p_added
                if start:
                    if counts(s - 1):
                        pe.wait_ge(x1_ready, s - 1)
                for j in range(4):
                    ins = mm(acc_ps[32 * j:32 * j + 32, i % 2, 0:PX], sel[:, :], prod[:, buf, j * PX:(j + 1) * PX],
                             start=start, stop=stop)
                ins.then_inc(done, 1)

            SEQ = [("w", 0, "S", 2), ("w", 0, "D", 4), ("w", 0, "D", 5), ("a", "D", 0), ("a", "D", 1),
                   ("w", 0, "S", 3), ("w", 0, "D", 6), ("t",), ("a", "P", 0), ("a", "D", 2),
                   ("w", 0, "D", 7), ("w", 0, "S", 4), ("a", "P", 1), ("a", "D", 3),
                   ("w", 1, "D", 0), ("g",), ("w", 1, "D", 1), ("a", "D", 4), ("a", "P", 2),
                   ("w", 1, "S", 0), ("w", 1, "D", 2), ("a", "D", 7),
                   ("w", 1, "S", 1), ("w", 1, "D", 3), ("a", "P", 3), ("a", "D", 6)]

            def image(b, first, last):
                for i in range(STEPS):
                    for e in SEQ:
                        if e[0] == "g":
                            if i == NK - 1 and not last:
                                group_mean(b + 1)
                            continue
                        if e[0] == "t":
                            if i >= NK and not last:
                                make_t(b + 1, i - NK)
                        elif e[0] == "a":
                            if e[1] == "D" and e[2] not in adds(i, last):
                                continue
                            add(b, i, e[1], e[2], e[1:] == ("D", 0), e[1:] == ("D", 6), last)
                        elif e[1] == 0:
                            make(b, i, e[2], e[3])
                        elif i + 1 < STEPS:
                            make(b, i + 1, e[2], e[3])
                        elif not last:
                            make(b + 1, 0, e[2], e[3])

            pe.wait_ge(const_in, 80)
            pe.wait_ge(w1_placed, 1)
            for h in range(2):
                ins = nc.tensor.transpose(acc_ps[:, 0, h * 128:(h + 1) * 128], w1_ordered[:, h * 128:(h + 1) * 128], ident[:, :])
            ins.then_inc(w1_ps, 1)
            group_mean(0)
            pe.wait_ge(w2_in, 16)
            for r in range(K):
                if counts(r - 3):
                    pe.wait_ge(w2_sb, r - 3)
                for c in range(K):
                    t = r * K + c
                    ins = nc.tensor.transpose(wt_ps[:, r % 4, c * G:(c + 1) * G], w2_raw[:, t * 128:(t + 1) * 128], ident[0:G, 0:G])
                ins.then_inc(w2_ps, 1)
            pe.wait_ge(w1_sb, 1)
            pe.wait_ge(ones_set, 1)
            for k in range(NK):
                if k == 5:
                    pe.wait_ge(abs_sum, 1)
                    mm(acc_ps[:, 0, 256:257], ones[:, :], cf[:, 24:25], start=True, stop=True).then_inc(abs_ps, 1)
                pe.wait_ge(norm_done, k + 1)
                if k >= 2:
                    pe.wait_ge(t_ready, k - 1)
                for h in range(2):
                    inner = xn_first[k % 4][:, h, :].rearrange("p (r c) -> p r c", c=PW)[:, :, PAD:PAD + HW]
                    ins = mm(first_bank(k), w1T[:, h, :], inner, start=h == 0, stop=h == 1)
                ins.then_inc(t_ps, 1)
            pe.wait_ge(b2_in, 32)
            for h in range(2):
                for q in range(13):
                    taps = quad_taps(q)
                    for j in range(4):
                        ins = mm(sb_ps[32 * j:32 * j + 32, h * 13 + q:h * 13 + q + 1],
                                 view(b2_row[h][:, taps[j]:taps[j] + 1], [[TAPS, 32]]), ones[0:1, 0:1], start=True, stop=True)
            ins.then_inc(b2_ps, 1)
            pe.wait_ge(wq_ready, 1)
            pe.wait_ge(ident_set, 1)
            pe.wait_ge(w2_sb, K)
            for r in range(5):
                if counts(r - 3):
                    pe.wait_ge(wq_sb, r - 3)
                for n in range(8 if r < 4 else 4):
                    o = (r * 8 + n) * 128
                    src = wq_ordered[:, o:o + 128]
                    ins = nc.tensor.transpose(wt_ps[:, r % 4, :].bitcast(bf16)[:, n * 128:(n + 1) * 128], src, ident_b)
                ins.then_inc(wq_ps, 1)
            pe.wait_ge(wq_sb, 5)
            pe.wait_ge(b2_sb, 1)
            for kind, n in ORDER[:AHEAD]:
                make(0, 0, kind, n)
            image(0, True, False)
            with pe.Fori(1, B - 1) as b:
                image(b, False, False)
            image(B - 1, False, True)

            NI = 2 * B
            small = raw[:, 1, 1, :]
            pe.wait_ge(gsum_in, 1)
            mm(misc_ps[:, 0:2 * NI], mask[:, :], raw[:, 0, 0, 64:64 + 2 * NI], start=True, stop=True).then_inc(gsum_ps, 1)
            pe.wait_ge(gsum_in, 3)
            for h in range(2):
                halves = view(raw[:, 0, 1, 6 * NI + h:6 * NI + h + 1], [[2, 2 * B]])
                ins = mm(misc_ps[:, 64:64 + 2 * B], ones[:, :], halves, start=h == 0, stop=h == 1)
            ins.then_inc(gsum_ps, 1)
            pe.wait_ge(gsum_in, 5)
            pe.wait_ge(ident_in, 16)
            mm(misc_ps[0:1, 128:256], small[:, 16:17], ident2, start=True, stop=True).then_inc(gsum_ps, 1)
            pe.wait_ge(gsum_in, 6)
            mm(misc_ps[:, 256:257], ones[0:1, :], small[0:1, 18:19], start=True, stop=True).then_inc(gsum_ps, 1)

            def conv(b, par):
                for n in range(TILES):
                    k, m = divmod(n, 2)
                    below = min(ROWS * (k + 1), HW - 1)
                    piece = [lo <= below < hi for lo, hi in pieces(b)].index(True)
                    if m == 0:
                        pe.wait_ge(q_ready, pieces_before(b) + 2 * piece + 2)
                    slot = (TILES * par + n) % 4
                    if counts(b * TILES + n - 3):
                        pe.wait_ge(y_scaled, b * TILES + n - 3)
                    c = 0
                    for kh in range(2):
                        src = xq(par)[:, kh, :].rearrange("p (r c) -> p r c", c=CW)
                        for tap in range(KK):
                            dy, dx = divmod(tap, 3)
                            o = ((m * 2 + kh) * KK + tap) * 128
                            ins = mm(conv_bank(slot), wqT[:, o:o + 128], src[:, ROWS * k + dy:ROWS * k + dy + ROWS, dx:dx + HW],
                                     start=c == 0, stop=c == 2 * KK - 1)
                            c += 1
                    ins.then_inc(conv_done, 1)

            pe.wait_ge(wq_in, 16)
            for par in range(2):
                conv(par, par)
            with pe.Fori(1, B // 2) as j:
                for par in range(2):
                    conv(j * 2 + par, par)


_INS = ["x", "L0_conv_w1", "L0_conv_b1", "L0_conv_w2", "L0_conv_b2", "L1_conv_weight", "L1_conv_bias",
        "L1_conv_ln_weight", "L1_conv_ln_bias"]


def kernel(**inputs):
    import numpy as _np
    import concourse.bacc as _bacc
    from concourse import mybir as _mybir
    from concourse.bass_utils import run_bass_kernel_spmd as _run

    nc = _bacc.Bacc("TRN2", target_bir_lowering=False, num_devices=1)
    part = _np.arange(128)
    shapes = {
        "ident": _np.eye(128, dtype=_np.float32),
        "sel": (part[:, None] % 32 == _np.arange(32)[None, :]).astype(_np.float32),
        "mask": ((part[:, None] % 32) // 2 == (part[None, :] % 32) // 2).astype(_np.float32) / 8,
    }
    arrays, args = {}, []
    for name, a in [(n, inputs[n]) for n in _INS] + list(shapes.items()):
        a = _np.ascontiguousarray(a)
        arrays[f"in_{name}"] = a
        args.append(nc.dram_tensor(f"in_{name}", a.shape, _mybir.dt.from_np(a.dtype), kind="ExternalInput").ap())
    args.append(nc.dram_tensor("out_y", (B, C, HW, HW), _mybir.dt.float32, kind="ExternalOutput").ap())
    build(nc, *args)
    r = _run(nc, [arrays], core_ids=[0])
    return r.results[0]["out_y"]
```
